# Optimizing a Trainium2 kernel written in Bass

```python
import numpy as np
import jax
import jax.numpy as jnp

def _softmax(x, axis=-1):
    return jax.nn.softmax(x, axis=axis)

def _gelu(x):
    return jax.nn.gelu(x, approximate=True)

def _silu(x):
    return jax.nn.silu(x)

def _sigmoid(x):
    return jax.nn.sigmoid(x)

def _layernorm(x, axis=-1, eps=1e-05):
    m = jnp.mean(x, axis=axis, keepdims=True)
    v = jnp.var(x, axis=axis, keepdims=True)
    return (x - m) / jnp.sqrt(v + eps)

def _scatter_add(tgt, idx, src, axis=0):
    return tgt.at[idx].add(src)

def _segment_sum(src, seg, n):
    return jax.ops.segment_sum(src, seg, n)
kernel_name = 'mk_adj_resnorm_d2_adj_r2_f394a6'

def setup_inputs(seed: int=0):
    np.random.seed(seed)
    _w = jnp.asarray

    def _rec_inputs():
        import jax
        import jax.numpy as jnp
        _gk = jax.random.key(seed)
        x = 7.22e-05 + 1 * jax.random.normal(jax.random.fold_in(_gk, 1), (8, 1024, 256), jnp.float32)
        _a = jax.random.bernoulli(jax.random.fold_in(_gk, 2), 0.015625, (8, 1024, 1024))
        _a = jnp.logical_or(_a, jnp.swapaxes(_a, -1, -2))
        _a = jnp.logical_or(_a, jnp.eye(1024, dtype=bool))
        adj = _a.astype(jnp.int32)
        return (x, adj)
    x, adj = _rec_inputs()

    def _L0_gnn_setup():
        import jax, jax.numpy as jnp
        import numpy as np
        B, N, DIN, DOUT = (8, 1024, 256, 256)
        key = jax.random.key(seed)
        kx, ka, kw, kb, kattn = jax.random.split(key, 5)
        x = jax.random.normal(kx, (B, N, DIN), dtype=jnp.float32)
        adjacency_matrix = jax.random.randint(ka, (B, N, N), 0, 2, dtype=jnp.int32)
        lim_w = float(np.sqrt(1.0 / DIN))
        W = jax.random.uniform(kw, (DOUT, DIN), minval=-lim_w, maxval=lim_w, dtype=jnp.float32)
        b = jax.random.uniform(kb, (DOUT,), minval=-lim_w, maxval=lim_w, dtype=jnp.float32)
        lim_a = float(np.sqrt(6.0 / (DOUT + DOUT)))
        attn = jax.random.uniform(kattn, (DOUT, DOUT), minval=-lim_a, maxval=lim_a, dtype=jnp.float32)
        return {'x': x, 'adjacency_matrix': adjacency_matrix, 'W': W, 'b': b, 'attn': attn}
    _L0_gnn_all = _L0_gnn_setup()
    _L0_gnn_in = {k: v for k, v in _L0_gnn_all.items() if k in ('W', 'b', 'attn')}
    del _L0_gnn_all

    def _L1_gnn_setup():
        import jax, jax.numpy as jnp
        import numpy as np
        L = 3
        D = 256
        B, N = (8, 512)
        EPS = 1e-05

        def layernorm(x, gamma, beta):
            mu = jnp.mean(x, axis=-1, keepdims=True)
            var = jnp.var(x, axis=-1, keepdims=True)
            return (x - mu) * jax.lax.rsqrt(var + EPS) * gamma + beta
        key = jax.random.key(seed)
        ks = jax.random.split(key, 12)
        s = 1.0 / np.sqrt(D)
        node_features = jax.random.normal(ks[0], (B, N, D), dtype=jnp.float32)
        adjacency_matrix = jax.random.randint(ks[1], (B, N, N), 0, 2, dtype=jnp.int32)
        return {'node_features': node_features, 'adjacency_matrix': adjacency_matrix, 'attn_w': jax.random.normal(ks[2], (L, 2 * D), dtype=jnp.float32) * (1.0 / np.sqrt(2 * D)), 'attn_b': jax.random.normal(ks[3], (L,), dtype=jnp.float32) * 0.01, 'W1': jax.random.normal(ks[4], (L, D, 4 * D), dtype=jnp.float32) * s, 'b1': jnp.zeros((L, 4 * D), dtype=jnp.float32), 'W2': jax.random.normal(ks[5], (L, 4 * D, D), dtype=jnp.float32) * (1.0 / np.sqrt(4 * D)), 'b2': jnp.zeros((L, D), dtype=jnp.float32), 'g1': jnp.ones((L, D), dtype=jnp.float32), 'beta1': jnp.zeros((L, D), dtype=jnp.float32), 'g2': jnp.ones((L, D), dtype=jnp.float32), 'beta2': jnp.zeros((L, D), dtype=jnp.float32)}
    _L1_gnn_all = _L1_gnn_setup()
    _L1_gnn_in = {k: v for k, v in _L1_gnn_all.items() if k in ('attn_w', 'attn_b', 'W1', 'b1', 'W2', 'b2', 'g1', 'beta1', 'g2', 'beta2')}
    del _L1_gnn_all
    return {'x': x, 'adj': adj, 'L0_gnn_W': _L0_gnn_in['W'], 'L0_gnn_b': _L0_gnn_in['b'], 'L0_gnn_attn': _L0_gnn_in['attn'], 'L1_gnn_attn_w': _L1_gnn_in['attn_w'], 'L1_gnn_attn_b': _L1_gnn_in['attn_b'], 'L1_gnn_W1': _L1_gnn_in['W1'], 'L1_gnn_b1': _L1_gnn_in['b1'], 'L1_gnn_W2': _L1_gnn_in['W2'], 'L1_gnn_b2': _L1_gnn_in['b2'], 'L1_gnn_g1': _L1_gnn_in['g1'], 'L1_gnn_beta1': _L1_gnn_in['beta1'], 'L1_gnn_g2': _L1_gnn_in['g2'], 'L1_gnn_beta2': _L1_gnn_in['beta2']}

def reference(x, adj, L0_gnn_W, L0_gnn_b, L0_gnn_attn, L1_gnn_attn_w, L1_gnn_attn_b, L1_gnn_W1, L1_gnn_b1, L1_gnn_W2, L1_gnn_b2, L1_gnn_g1, L1_gnn_beta1, L1_gnn_g2, L1_gnn_beta2):
    import jax
    import jax.numpy as jnp

    def _L0_gnn_ref(x, adjacency_matrix, W, b, attn):
        import jax, jax.numpy as jnp
        import numpy as np
        B, N, DIN, DOUT = (8, 1024, 256, 256)
        h = jnp.einsum('bni,oi->bno', x, W) + b
        ha = jnp.einsum('bmi,ij->bmj', h, attn)
        scores = jnp.einsum('bmj,bnj->bmn', ha, h)
        scores = jnp.where(adjacency_matrix == 0, -jnp.inf, scores)
        attn_weights = jax.nn.softmax(scores, axis=-1)
        x_out = jnp.einsum('bmn,bnd->bmd', attn_weights, h)
        return jax.nn.elu(x_out)

    def _L1_gnn_ref(node_features, adjacency_matrix, attn_w, attn_b, W1, b1, W2, b2, g1, beta1, g2, beta2):
        import jax, jax.numpy as jnp
        import numpy as np
        L = 3
        D = 256
        B, N = (8, 512)
        EPS = 1e-05

        def layernorm(x, gamma, beta):
            mu = jnp.mean(x, axis=-1, keepdims=True)
            var = jnp.var(x, axis=-1, keepdims=True)
            return (x - mu) * jax.lax.rsqrt(var + EPS) * gamma + beta
        n = adjacency_matrix.shape[-1]
        mask = adjacency_matrix.astype(jnp.float32) + jnp.eye(n, dtype=jnp.float32) > 0
        x = node_features
        d = x.shape[-1]
        for l in range(attn_w.shape[0]):
            si = x @ attn_w[l, :d]
            sj = x @ attn_w[l, d:]
            scores = si[:, :, None] + sj[:, None, :] + attn_b[l]
            scores = jnp.where(scores >= 0, scores, 0.2 * scores)
            scores = jnp.where(mask, scores, -jnp.inf)
            attn = jax.nn.softmax(scores, axis=-1)
            agg = jnp.einsum('bij,bjd->bid', attn, x)
            h = layernorm(x + agg, g1[l], beta1[l])
            ff = jax.nn.gelu(h @ W1[l] + b1[l], approximate=False) @ W2[l] + b2[l]
            x = layernorm(h + ff, g2[l], beta2[l])
        return x
    x = _layernorm(x + _L0_gnn_ref(x, adj, L0_gnn_W, L0_gnn_b, L0_gnn_attn), axis=-1)
    x = _layernorm(x + _L1_gnn_ref(x, adj, L1_gnn_attn_w, L1_gnn_attn_b, L1_gnn_W1, L1_gnn_b1, L1_gnn_W2, L1_gnn_b2, L1_gnn_g1, L1_gnn_beta1, L1_gnn_g2, L1_gnn_beta2), axis=-1)
    return x

_drawn_inputs = setup_inputs


def setup_inputs(seed=0):
    import zlib

    import numpy as np

    out = dict(_drawn_inputs(seed))
    spreads = {'L1_gnn_b1': (0.0, 0.1),
     'L1_gnn_b2': (0.0, 0.1),
     'L1_gnn_g1': (1.0, 0.2),
     'L1_gnn_beta1': (0.0, 0.1),
     'L1_gnn_g2': (1.0, 0.2),
     'L1_gnn_beta2': (0.0, 0.1)}
    factors = {'L1_gnn_attn_b': 194.97}
    for name, (base, spread) in spreads.items():
        noise = np.random.default_rng([zlib.crc32(name.encode()), seed]).standard_normal(out[name].shape)
        drawn = base * np.exp(spread * noise) if base else spread * noise
        out[name] = jnp.asarray(drawn.astype(out[name].dtype))
    for name, factor in factors.items():
        out[name] = (out[name] * factor).astype(out[name].dtype)
    return out
```

```python
from contextlib import ExitStack

import concourse.bass as bass
from concourse import mybir


P = 128
F32 = mybir.dt.float32
F32R = mybir.dt.float32r
BF16 = mybir.dt.bfloat16
I32 = mybir.dt.int32
ALU = mybir.AluOpType
ACT = mybir.ActivationFunctionType

MASKED = -1.0e30
LOWEST = -3.0e38
EPS = 1e-5
SLOPE = 0.2
BANK = 512


def shapes(x, w1):
    B, N, D = x.shape
    F = w1.shape[2]
    return B, N, D, F, N // P, D // P, F // P


def split_product(pe, out, hi_lo_left, hi_lo_right, start, stop):
    (left_hi, left_lo), (right_hi, right_lo) = hi_lo_left, hi_lo_right
    pe.matmul(out, left_hi, right_hi, start=start, stop=False)
    pe.matmul(out, left_lo, right_hi, start=False, stop=False)
    return pe.matmul(out, left_hi, right_lo, start=False, stop=stop)


def wait_alone(eng, passed, *waits):
    for sem, value in waits:
        eng.wait_ge(sem, value)
    eng.sem_inc(passed, 1)


def make_identity(pool, ident, done):
    pool.memset(ident[:, :], 0.0).then_inc(done, 1)
    pool.wait_ge(done, 1)
    pool.affine_select(out=ident[:, :], in_=ident[:, :], compare_op=ALU.not_equal, fill=1.0,
                       base=0, pattern=[[-1, P]], channel_multiplier=1).then_inc(done, 1)


def first_stage(nc, x, adj, W, bias, attn, x1_dram, mask_dram, w1):
    B, N, D, _, NT, KD, _ = shapes(x, w1)
    NC = N // BANK
    TC = BANK // P
    DE = D + 2
    AR = 4
    PJ = 4 * NC * KD
    with ExitStack() as ctx:
        def sb(name, shape, dt=F32):
            return ctx.enter_context(nc.sbuf_tensor("a_" + name, shape, dt))

        def sem(name):
            return ctx.enter_context(nc.semaphore("a_" + name))

        ident = sb("ident", [P, P])
        ident_r = sb("ident_r", [P, P], F32R)
        w_in = sb("w_in", [P, KD, D])
        at_in = sb("at_in", [P, KD, D])
        bias_col = sb("bias_col", [P, KD])
        wT = [sb("wT_hi", [P, KD, D], F32R), sb("wT_lo", [P, KD, D], F32R)]
        at = [sb("at_hi", [P, KD, D], F32R), sb("at_lo", [P, KD, D], F32R)]
        xs = sb("xs", [P, NT, D])
        xr = sb("xr", [P, NT, D])
        xT = [sb("xT_hi", [P, KD, N], F32R), sb("xT_lo", [P, KD, N], F32R)]
        hT = [sb("hT_hi", [P, KD, N], F32R), sb("hT_lo", [P, KD, N], F32R)]
        haT = [sb("haT_hi", [P, KD, N], F32R), sb("haT_lo", [P, KD, N], F32R)]
        hn = [sb("hn_hi", [P, NT, DE], F32R), sb("hn_lo", [P, NT, D], F32R)]
        adj_t = sb("adj_t", [P, AR, N], I32)
        mask0 = sb("mask0", [P, 2, N], BF16)
        mask1 = sb("mask1", [P, 2, N], BF16)
        t = [sb(f"t{i}", [P, N]) for i in range(2)]
        pT = [[sb(f"pT_hi{i}", [P, N], F32R), sb(f"pT_lo{i}", [P, N], F32R)] for i in range(2)]
        mx = sb("mx", [P, 2])
        nmx = sb("nmx", [P, 2])
        rinv = sb("rinv", [P, 1])
        neg = sb("neg", [P, 2, D])
        y = sb("y", [P, 2, D])
        stats = sb("stats", [P, 2, 6])
        mv = sb("mv", [P, 2, 2])
        ve = sb("ve", [P, 2])
        rstd = sb("rstd", [P, 2])
        half = sb("half", [P, 1])
        eps = sb("eps", [P, 1])
        xo = sb("xo", [P, 2, D])

        S = [ctx.enter_context(nc.psum_tensor(f"a_S{i}", [P, N], F32)) for i in range(2)]
        PT = ctx.enter_context(nc.psum_tensor("a_PT", [P, N], F32))
        O = [ctx.enter_context(nc.psum_tensor(f"a_O{i}", [P, BANK], F32)) for i in range(2)]
        pj_bank = [S[0][:, 0:BANK], S[0][:, BANK:N]]

        s_id = sem("ident")
        s_idr = sem("ident_r")
        s_half = sem("half")
        s_ones = sem("ones")
        s_w = sem("weights_in")
        s_wt = sem("w_transposed")
        s_whi = sem("weights_hi")
        s_wlo = sem("weights_lo")
        s_xs = sem("xs_in")
        s_xr = sem("xr_in")
        s_adj = [sem(f"adj_in{i}") for i in range(AR)]
        s_mask = sem("mask_step")
        s_mst = [sem(f"mask_stored{i}") for i in range(2)]
        s_mm = sem("proj_product")
        s_phi = sem("proj_hi")
        s_plo = sem("proj_lo")
        s_s = sem("scores")
        s_t = sem("masked")
        s_nm = sem("max_negated")
        s_p = sem("probs")
        s_tr = sem("probs_transposed")
        s_thi = sem("probsT_hi")
        s_tlo = sem("probsT_lo")
        s_pv = sem("values")
        s_ln = sem("norm_step")
        s_ex = sem("elu_exp")
        s_passed = sem("passed")
        s_rs = sem("rstd_step")
        s_st = [sem(f"x1_stored{i}") for i in range(2)]
        LN = 8

        block = ctx.enter_context(nc.Block())

        @block.sync
        def _(sp):
            sp.dma_start(w_in[:, :, :], W.rearrange("(k p) i -> p k i", p=P)).then_inc(s_w, 16)
            sp.dma_start(at_in[:, :, :], attn.rearrange("(k p) j -> p k j", p=P)).then_inc(s_w, 16)
            with nc.allow_non_contiguous_dma("a column of the bias"):
                sp.dma_start(bias_col[:, :], bias.rearrange("(k p) -> p k", p=P)).then_inc(s_w, 16)
            sp.dma_start(xs[:, :, :], x[0].rearrange("(t p) d -> p t d", p=P)).then_inc(s_xs, 16)

            def batch(b, first):
                for k in range(NT):
                    if not (first and k < AR):
                        sp.wait_ge(s_mask, 3 * (NT * b + k - AR + 1))
                    sp.dma_start(adj_t[:, k % AR, :], adj[b, k * P:(k + 1) * P, :]).then_inc(s_adj[k % AR], 16)
                    if k == 1:
                        if not first:
                            sp.wait_ge(s_ln, LN * (NT * b - 1) + 4)
                        sp.dma_start(xr[:, :, :], x[b].rearrange("(t p) d -> p t d", p=P)).then_inc(s_xr, 16)
                    if k == 3:
                        sp.wait_ge(s_mm, PJ * b + NC * KD)
                        sp.dma_start(xs[:, :, :], x[(b + 1) % B].rearrange("(t p) d -> p t d", p=P)).then_inc(s_xs, 16)
                    if k >= 3:
                        store_mask(b, k - 3)
                    if k >= 5:
                        store_x1(b, k - 5)
                for k in range(NT - 3, NT):
                    store_mask(b, k)
                    store_x1(b, k - 2)
                for k in range(NT - 2, NT):
                    store_x1(b, k)

            def store_mask(b, k):
                sp.wait_ge(s_mask, 3 * (NT * b + k + 1))
                sp.dma_start(mask_dram[b * NT + k], mask1[:, k % 2, :]).then_inc(s_mst[k % 2], 16)

            def store_x1(b, k):
                sp.wait_ge(s_ln, LN * (NT * b + k + 1))
                sp.dma_start(x1_dram[b * NT + k], xo[:, k % 2, :]).then_inc(s_st[k % 2], 16)

            batch(0, True)
            with sp.Fori(1, B) as b:
                batch(b, False)
            for i in range(2):
                sp.wait_ge(s_mst[i], 16 * B * NT // 2)
                sp.wait_ge(s_st[i], 16 * B * NT // 2)
            sp.wait_ge(s_xs, 16 * (B + 1))

        @block.gpsimd
        def _(pool):
            make_identity(pool, ident, s_id)
            pool.memset(half[:, :], -0.5).then_inc(s_half, 1)
            pool.memset(eps[:, :], EPS).then_inc(s_half, 1)
            pool.memset(hn[0][:, :, D:D + 1].bitcast(F32), 1.0).then_inc(s_ones, 1)
            pool.memset(hn[0][:, :, D + 1:DE].bitcast(F32), 0.0).then_inc(s_ones, 1)
            pool.wait_ge(s_half, 2)

            def batch(b):
                for k in range(NT):
                    n = NT * b + k
                    i = k % 2
                    pool.wait_ge(s_ln, LN * n + 7)
                    pool.tensor_tensor(ve[:, i:i + 1], mv[:, i, 1:2], eps[:, :], ALU.add).then_inc(s_rs, 1)
                    pool.wait_ge(s_rs, 2 * n + 1)
                    pool.tensor_tensor(rstd[:, i:i + 1], ve[:, i:i + 1], half[:, :], ALU.pow).then_inc(s_rs, 1)

            with pool.Fori(0, B) as b:
                batch(b)

        @block.scalar
        def _(act):
            act.wait_ge(s_w, 48)
            act.activation(at[0][:, :, :], at_in[:, :, :], ACT.Copy).then_inc(s_whi, 1)
            act.wait_ge(s_wt, KD * KD)
            for k in range(KD):
                act.activation(wT[0][:, k, :], PT[:, k * BANK:k * BANK + D], ACT.Copy).then_inc(s_whi, 1)

            def proj_hi(b, p):
                part, c, k = p // (NC * KD), p % (NC * KD) // KD, p % KD
                act.wait_ge(s_mm, PJ * b + p + 1)
                src = pj_bank[p % 2]
                cs = slice(c * BANK, (c + 1) * BANK)
                if part == 0:
                    act.activation(xT[0][:, k, cs], src, ACT.Copy).then_inc(s_phi, 1)
                elif part == 1:
                    act.activation(hT[0][:, k, cs], src, ACT.Identity, bias=bias_col[:, k:k + 1]).then_inc(s_phi, 1)
                elif part == 2:
                    act.activation(haT[0][:, k, cs], src, ACT.Copy).then_inc(s_phi, 1)
                else:
                    g = p % (NC * KD)
                    act.activation(hn[0][:, 2 * g:2 * g + 2, 0:D], src.rearrange("p (t d) -> p t d", d=D),
                                   ACT.Copy).then_inc(s_phi, 1)

            def softmax_exp(b, k):
                act.wait_ge(s_nm, NT * b + k + 1)
                act.activation(t[k % 2][:, :], t[k % 2][:, :], ACT.Exp, bias=nmx[:, k % 2:k % 2 + 1]).then_inc(s_p, 1)

            def transposed_hi(b, k, first):
                if not (first and k < 2):
                    act.wait_ge(s_pv, NT * b + k - 1)
                for g in range(2):
                    act.wait_ge(s_tr, 2 * (NT * b + k) + g + 1)
                    gs = slice(g * BANK, (g + 1) * BANK)
                    act.activation(pT[k % 2][0][:, gs], PT[:, gs], ACT.Copy).then_inc(s_thi, 1)

            def batch(b, first):
                for p in range(PJ):
                    proj_hi(b, p)
                softmax_exp(b, 0)
                softmax_exp(b, 1)
                transposed_hi(b, 0, first)
                for k in range(NT):
                    if k + 1 < NT:
                        transposed_hi(b, k + 1, first)
                    if k + 2 < NT:
                        softmax_exp(b, k + 2)
                    act.wait_ge(s_ln, LN * (NT * b + k) + 3)
                    act.activation(neg[:, k % 2, :], neg[:, k % 2, :], ACT.Exp).then_inc(s_ex, 1)

            batch(0, True)
            with act.Fori(1, B) as b:
                batch(b, False)

        @block.vector
        def _(dve):
            dve.wait_ge(s_id, 2)
            dve.tensor_copy(ident_r[:, :], ident[:, :]).then_inc(s_idr, 1)
            dve.wait_ge(s_whi, 1)
            dve.tensor_tensor(at[1][:, :, :], at_in[:, :, :], at[0][:, :, :].bitcast(F32), ALU.subtract).then_inc(s_wlo, 1)
            for k in range(KD):
                dve.wait_ge(s_whi, 2 + k)
                dve.tensor_tensor(wT[1][:, k, :], PT[:, k * BANK:k * BANK + D], wT[0][:, k, :].bitcast(F32),
                                  ALU.subtract).then_inc(s_wlo, 1)

            def proj_lo(b, p):
                part, c, k = p // (NC * KD), p % (NC * KD) // KD, p % KD
                dve.wait_ge(s_phi, PJ * b + p + 1)
                src = pj_bank[p % 2]
                cs = slice(c * BANK, (c + 1) * BANK)
                if part == 0:
                    dve.tensor_tensor(xT[1][:, k, cs], src, xT[0][:, k, cs].bitcast(F32), ALU.subtract).then_inc(s_plo, 1)
                elif part == 1:
                    dve.scalar_tensor_tensor(hT[1][:, k, cs], src, bias_col[:, k:k + 1], hT[0][:, k, cs].bitcast(F32),
                                             ALU.add, ALU.subtract).then_inc(s_plo, 1)
                elif part == 2:
                    dve.tensor_tensor(haT[1][:, k, cs], src, haT[0][:, k, cs].bitcast(F32), ALU.subtract).then_inc(s_plo, 1)
                else:
                    g = p % (NC * KD)
                    dve.tensor_tensor(hn[1][:, 2 * g:2 * g + 2, :], src.rearrange("p (t d) -> p t d", d=D),
                                      hn[0][:, 2 * g:2 * g + 2, 0:D].bitcast(F32), ALU.subtract).then_inc(s_plo, 1)

            def masks(b, k, first):
                n = NT * b + k
                i, a = k % 2, k % AR
                dve.wait_ge(s_adj[a], 16 * (NT // AR * b + k // AR + 1))
                dve.tensor_scalar(mask0[:, i, :], adj_t[:, a, :], 0.0, MASKED, ALU.is_equal, ALU.mult).then_inc(s_mask, 1)
                dve.wait_ge(s_mask, 3 * n + 1)
                dg = adj_t[:, a, k * P:(k + 1) * P]
                dve.tensor_tensor(dg, dg, ident[:, :], ALU.add).then_inc(s_mask, 1)
                dve.wait_ge(s_mask, 3 * n + 2)
                if not (first and k < 2):
                    dve.wait_ge(s_mst[i], 16 * (NT // 2 * b + k // 2))
                dve.tensor_scalar(mask1[:, i, :], adj_t[:, a, :], 0.0, MASKED, ALU.is_le, ALU.mult).then_inc(s_mask, 1)

            def masked_scores(b, k, first):
                n = NT * b + k
                i = k % 2
                if first and k < 2:
                    dve.wait_ge(s_s, n + 1)
                else:
                    wait_alone(dve, s_passed, (s_s, n + 1), (s_tr, 2 * (n - 1)))
                dve.tensor_tensor_reduce(out=t[i][:, :], in0=S[i][:, :], in1=mask0[:, i, :], scale=1.0, scalar=LOWEST,
                                         op0=ALU.add, op1=ALU.max, accum_out=mx[:, i:i + 1]).then_inc(s_t, 1)
                dve.wait_ge(s_t, n + 1)
                dve.tensor_scalar(nmx[:, i:i + 1], mx[:, i:i + 1], -1.0, None, ALU.mult).then_inc(s_nm, 1)

            def transposed_lo(b, k):
                for g in range(2):
                    dve.wait_ge(s_thi, 2 * (NT * b + k) + g + 1)
                    gs = slice(g * BANK, (g + 1) * BANK)
                    dve.tensor_tensor(pT[k % 2][1][:, gs], PT[:, gs], pT[k % 2][0][:, gs].bitcast(F32),
                                      ALU.subtract).then_inc(s_tlo, 1)

            def elu_norm(b, k, first):
                n = NT * b + k
                i = k % 2
                o = O[i][:, 0:D]
                dve.wait_ge(s_pv, n + 1)
                dve.reciprocal(rinv[:, :], O[i][:, D:D + 1]).then_inc(s_ln, 1)
                dve.wait_ge(s_ln, LN * n + 1)
                dve.tensor_scalar(y[:, i, :], o, rinv[:, :], 0.0, ALU.mult, ALU.max).then_inc(s_ln, 1)
                dve.tensor_scalar(neg[:, i, :], o, rinv[:, :], 0.0, ALU.mult, ALU.min).then_inc(s_ln, 1)
                if k == 0:
                    dve.wait_ge(s_xr, 16 * (b + 1))
                dve.wait_ge(s_ln, LN * n + 2)
                dve.scalar_tensor_tensor(y[:, i, :], y[:, i, :], -1.0, xr[:, k, :], ALU.add, ALU.add).then_inc(s_ln, 1)

            def elu_norm2(b, k, first):
                n = NT * b + k
                i = k % 2
                dve.wait_ge(s_ln, LN * n + 4)
                dve.wait_ge(s_ex, n + 1)
                dve.tensor_tensor(y[:, i, :], y[:, i, :], neg[:, i, :], ALU.add).then_inc(s_ln, 1)
                dve.wait_ge(s_ln, LN * n + 5)
                dve.bn_stats(stats[:, i, :], y[:, i, :]).then_inc(s_ln, 1)
                wait_alone(dve, s_passed, (s_ln, LN * n + 6))
                dve.bn_aggr(mv[:, i, :], stats[:, i, :]).then_inc(s_ln, 1)
                dve.wait_ge(s_rs, 2 * n + 2)
                if not (first and k < 2):
                    dve.wait_ge(s_st[i], 16 * (NT // 2 * b + k // 2))
                dve.tensor_scalar(xo[:, i, :], y[:, i, :], mv[:, i, 0:1], rstd[:, i:i + 1], ALU.subtract,
                                  ALU.mult).then_inc(s_ln, 1)

            def batch(b, first):
                masks(b, 0, first)
                for p in range(PJ):
                    proj_lo(b, p)
                masks(b, 1, first)
                masked_scores(b, 0, first)
                masked_scores(b, 1, first)
                masks(b, 2, first)
                transposed_lo(b, 0)
                for k in range(NT):
                    if k + 1 < NT:
                        transposed_lo(b, k + 1)
                    if k + 2 < NT:
                        masked_scores(b, k + 2, first)
                    elu_norm(b, k, first)
                    if k + 3 < NT:
                        masks(b, k + 3, first)
                    elu_norm2(b, k, first)

            batch(0, True)
            with dve.Fori(1, B) as b:
                batch(b, False)

        @block.tensor
        def _(pe):
            pe.wait_ge(s_id, 2)
            pe.wait_ge(s_w, 48)
            for k in range(KD):
                for o in range(KD):
                    pe.transpose(PT[:, k * BANK + o * P:k * BANK + (o + 1) * P], w_in[:, o, k * P:(k + 1) * P],
                                 ident[:, :]).then_inc(s_wt, 1)
            pe.wait_ge(s_idr, 1)
            pe.wait_ge(s_wlo, 1 + KD)
            pe.wait_ge(s_ones, 2)

            def bank_free(b, p, first):
                if p >= 2:
                    pe.wait_ge(s_plo, PJ * b + p - 1)
                elif not first:
                    pe.wait_ge(s_t, NT * b)

            def projections(b, first):
                pe.wait_ge(s_xs, 16 * (b + 1))
                p = 0
                for c in range(NC):
                    for k in range(KD):
                        bank_free(b, p, first)
                        for q in range(TC):
                            mm = pe.transpose(pj_bank[p % 2][:, q * P:(q + 1) * P],
                                              xs[:, TC * c + q, k * P:(k + 1) * P], ident[:, :])
                        mm.then_inc(s_mm, 1)
                        p += 1
                for src, w, parts in ((xT, wT, 0), (hT, at, 1)):
                    for c in range(NC):
                        cs = slice(c * BANK, (c + 1) * BANK)
                        pe.wait_ge(s_plo, PJ * b + NC * KD * parts + KD * (c + 1))
                        for o in range(KD):
                            bank_free(b, p, first)
                            os = slice(o * P, (o + 1) * P)
                            for k in range(KD):
                                mm = split_product(pe, pj_bank[p % 2], (w[0][:, k, os], w[1][:, k, os]),
                                                   (src[0][:, k, cs], src[1][:, k, cs]), k == 0, k == KD - 1)
                            mm.then_inc(s_mm, 1)
                            p += 1
                for g in range(NT // 2):
                    bank_free(b, p, first)
                    for q in range(2):
                        ts = slice((2 * g + q) * P, (2 * g + q + 1) * P)
                        for k in range(KD):
                            out = pj_bank[p % 2][:, q * D + k * P:q * D + (k + 1) * P]
                            pe.matmul(out, hT[0][:, k, ts], ident_r[:, :], start=True, stop=False)
                            mm = pe.matmul(out, hT[1][:, k, ts], ident_r[:, :], start=False, stop=True)
                    mm.then_inc(s_mm, 1)
                    p += 1
                assert p == PJ

            def scores(b, j, first):
                n = NT * b + j
                if j >= 2:
                    pe.wait_ge(s_t, n - 1)
                elif j == 1 and not first:
                    pe.wait_ge(s_t, n - 1)
                ts = slice(j * P, (j + 1) * P)
                for c in range(NC):
                    cs = slice(c * BANK, (c + 1) * BANK)
                    for k in range(KD):
                        mm = split_product(pe, S[j % 2][:, cs], (haT[0][:, k, ts], haT[1][:, k, ts]),
                                           (hT[0][:, k, cs], hT[1][:, k, cs]), k == 0, k == KD - 1)
                mm.then_inc(s_s, 1)

            def transpose_probs(b, j, first):
                n = NT * b + j
                pe.wait_ge(s_p, n + 1)
                for g in range(2):
                    if not (first and j == 0):
                        pe.wait_ge(s_tlo, 2 * n - 1 + g)
                    for q in range(TC):
                        js = slice((TC * g + q) * P, (TC * g + q + 1) * P)
                        mm = pe.transpose(PT[:, js], t[j % 2][:, js], ident[:, :])
                    mm.then_inc(s_tr, 1)

            def values(b, k, first):
                n = NT * b + k
                pe.wait_ge(s_tlo, 2 * n + 2)
                if not (first and k < 2):
                    pe.wait_ge(s_ln, LN * (n - 2) + 3)
                for j in range(NT):
                    js = slice(j * P, (j + 1) * P)
                    pe.matmul(O[k % 2][:, 0:DE], pT[k % 2][0][:, js], hn[0][:, j, :], start=(j == 0), stop=False)
                    pe.matmul(O[k % 2][:, 0:DE], pT[k % 2][1][:, js], hn[0][:, j, :], start=False, stop=False)
                    mm = pe.matmul(O[k % 2][:, 0:D], pT[k % 2][0][:, js], hn[1][:, j, :], start=False, stop=(j == NT - 1))
                mm.then_inc(s_pv, 1)

            def batch(b, first):
                projections(b, first)
                pe.wait_ge(s_plo, PJ * (b + 1))
                scores(b, 0, first)
                scores(b, 1, first)
                transpose_probs(b, 0, first)
                for k in range(NT):
                    if k + 2 < NT:
                        scores(b, k + 2, first)
                    if k + 1 < NT:
                        transpose_probs(b, k + 1, first)
                    values(b, k, first)

            batch(0, True)
            with pe.Fori(1, B) as b:
                batch(b, False)


class Layers:
    pass


def layer_buffers(nc, ctx, x, w1):
    B, N, D, F, NT, KD, KF = shapes(x, w1)
    L = Layers()

    def sb(name, shape, dt=F32):
        return ctx.enter_context(nc.sbuf_tensor(name, shape, dt))

    def ps(name, cols):
        return ctx.enter_context(nc.psum_tensor(name, [P, cols], F32))

    def sem(name):
        return ctx.enter_context(nc.semaphore(name))

    DE = D + 2
    TC = BANK // P
    L.ident = sb("ident", [P, P])
    L.half = sb("half", [P, TC])
    L.eps = sb("eps", [P, TC])
    L.w1 = [sb("w1_hi", [P, KD, F], F32R), sb("w1_lo", [P, KD, F], F32R)]
    L.w2 = [sb("w2_hi", [P, KF, D], F32R), sb("w2_lo", [P, KF, D], F32R)]
    L.b1 = sb("b1", [P, KF])
    L.b2 = sb("b2", [P, KD])
    L.g1 = sb("g1", [P, KD])
    L.be1 = sb("be1", [P, KD])
    L.g2 = sb("g2", [P, D])
    L.be2 = sb("be2", [P, D])
    L.aw = sb("aw", [P, 2, D])
    L.ab = sb("ab", [P, 1])
    L.mask = [sb(f"mask{i}", [P, N], BF16) for i in range(TC)]
    L.x = sb("x", [P, 2, NT, D])
    L.x_hi = sb("x_hi", [P, 2, NT, DE], F32R)
    L.x_lo = sb("x_lo", [P, 2, NT, D], F32R)
    L.prod = sb("prod", [P, 4, D])
    L.si = sb("si", [P, NT])
    L.sj = sb("sj", [P, NT])
    L.a4 = sb("a4", [P, NT])
    L.am = sb("am", [P, NT])
    L.sj_row = sb("sj_row", [P, N])
    L.t = [sb(f"t{i}", [P, N]) for i in range(2)]
    L.r = [sb(f"r{i}", [P, N]) for i in range(2)]
    L.mx = sb("mx", [P, 2])
    L.mp = sb("mp", [P, 2])
    L.c2 = sb("c2", [P, TC])
    L.pT = [[sb(f"pT_hi{i}", [P, N], F32R), sb(f"pT_lo{i}", [P, N], F32R)] for i in range(2)]
    L.rinv = sb("rinv", [P, 1])
    L.u = sb("u", [P, 2, D])
    L.st = sb("st", [P, 2, 6])
    L.mv = sb("mv", [P, 2, 2])
    L.ve = sb("ve", [P, 2])
    L.rstd = sb("rstd", [P, 2])
    L.n1 = sb("n1", [P, 2, TC, D])
    L.h = sb("h", [P, KD, BANK])
    L.h_hi = sb("h_hi", [P, KD, BANK], F32R)
    L.h_lo = sb("h_lo", [P, KD, BANK], F32R)
    L.g = sb("g", [P, 2, BANK])
    L.g_hi = sb("g_hi", [P, KF, BANK], F32R)
    L.g_lo = sb("g_lo", [P, KF, BANK], F32R)
    L.rT = sb("rT", [P, KD, BANK])
    L.st2 = sb("st2", [P, TC, 6])
    L.mv2 = sb("mv2", [P, TC, 2])
    L.ve2 = sb("ve2", [P, TC])
    L.rstd2 = sb("rstd2", [P, TC])
    L.xo = sb("xo", [P, TC, D])
    L.x1 = sb("x1", [P, TC, D])

    L.PT = ps("PT", N)
    L.A = ps("A", BANK)
    L.G = [ps(f"G{i}", BANK) for i in range(2)]
    L.Y = ps("Y", BANK)
    L.M = ps("M", 2 * BANK)

    L.s_ident = sem("ident")
    L.s_half = sem("half")
    L.s_ones = sem("ones")
    L.s_w_in = sem("w_in")
    L.s_w_hi = sem("w_hi")
    L.s_w_lo = sem("w_lo")
    L.s_x_in = sem("x_in")
    L.s_x_hi = sem("x_hi")
    L.s_x_lo = sem("x_lo")
    L.s_sj = sem("sj")
    L.s_prep = sem("prep")
    L.s_sjT = sem("sjT")
    L.s_sj_row = sem("sj_row")
    L.s_masked = sem("masked")
    L.s_max_step = sem("max_step")
    L.s_relu = sem("relu")
    L.s_sadd = sem("sadd")
    L.s_probs = sem("probs")
    L.s_tr = sem("tr")
    L.s_pt_hi = sem("pt_hi")
    L.s_pt_lo = sem("pt_lo")
    L.s_agg = sem("agg")
    L.s_ln = sem("ln")
    L.s_rs = sem("rs")
    L.s_n1 = sem("n1")
    L.s_hT = sem("hT")
    L.s_h = sem("h")
    L.s_h_lo = sem("h_lo")
    L.s_ffn1 = sem("ffn1")
    L.s_gelu = sem("gelu")
    L.s_g_hi = sem("g_hi")
    L.s_g_lo = sem("g_lo")
    L.s_ffn2 = sem("ffn2")
    L.s_res = sem("res")
    L.s_rt = sem("rt")
    L.s_ln2 = sem("ln2")
    L.s_rs2 = sem("rs2")
    L.s_n2 = sem("n2")
    L.s_xo = sem("xo")
    L.s_xst = sem("xst")
    L.s_x1_in = sem("x1_in")
    L.s_fin = sem("fin")
    L.s_passed = sem("passed")
    L.s_mask = [sem(f"mask_in{i}") for i in range(TC)]
    return L


def graph_layer(nc, L, layer, x, x_in, x_out, x1, mask, par, last):
    aw, ab, W1, b1, W2, b2, g1, be1, g2, be2 = par
    B, N, D, F, NT, KD, KF = shapes(x, W1)
    DE, TC = D + 2, BANK // P
    NCH = N // BANK
    C = B * NCH
    U = B * NT
    assert NCH == 2 and NT == NCH * TC and KF == NT
    u_prep, u_tr, n_batch = layer * (U + 2), layer * (U + 1), layer * (B + 1)
    u0, c0, m0 = layer * U, layer * C, layer * (U + TC) // TC

    def rs2(c, final):
        return 2 * c0 + (4 * c + 2 * final if last else 2 * c)

    def batches(emit, loop):
        for b in range(2):
            for h in range(NCH):
                c = NCH * b + h
                emit(b, h, True, c >= 1, c >= 2, last and c >= 3)
        with loop(2, B) as b:
            for h in range(NCH):
                emit(b, h, True, True, True, last)
        emit(B, 0, False, True, True, last)
        emit(B, 1, False, False, True, last)
        if last:
            emit(B + 1, 0, False, False, False, True)

    with nc.Block() as block:
        @block.sync
        def _(sp):
            stage = [L.t[0], L.t[1], L.r[0], L.r[1]]
            for k in range(KD):
                sp.dma_start(stage[k][:, :], W1[layer, k * P:(k + 1) * P, :]).then_inc(L.s_w_in, 16)
            w2 = W2[layer].rearrange("(f p) d -> p f d", p=P)
            for k in range(KD):
                fs = slice(k * KF // KD, (k + 1) * KF // KD)
                sp.dma_start(stage[KD + k][:, :].rearrange("p (f d) -> p f d", d=D), w2[:, fs, :]).then_inc(L.s_w_in, 16)
            with nc.allow_non_contiguous_dma("columns of the layer's vectors"):
                for dst, src in ((L.b1, b1), (L.b2, b2), (L.g1, g1), (L.be1, be1)):
                    sp.dma_start(dst[:, :], src[layer].rearrange("(k p) -> p k", p=P)).then_inc(L.s_w_in, 16)
                for dst, src in ((L.g2[:, :], g2[layer]), (L.be2[:, :], be2[layer]), (L.aw[:, 0, :], aw[layer, 0:D]),
                                 (L.aw[:, 1, :], aw[layer, D:2 * D]), (L.ab[:, :], ab[layer:layer + 1])):
                    sp.dma_start(dst, src.partition_broadcast(P)).then_inc(L.s_w_in, 16)

            def load_x(b, par):
                rows = x_in[bass.ds(b * NCH, NCH)]
                sp.dma_start(L.x[:, par, :, :].rearrange("p (c t) d -> p c t d", c=NCH),
                             rows.rearrange("c p t d -> p c t d")).then_inc(L.s_x_in, 16)

            def load_mask(b, s):
                sp.dma_start(L.mask[s % TC][:, :], mask[b * NT + s % NT]).then_inc(L.s_mask[s % TC], 16)

            load_x(0, 0)
            for s in range(TC):
                load_mask(0, s)

            def emit(b, h, att, ffn, rt, fin):
                u, c = NT * b + TC * h, NCH * b + h
                if att and h == 0:
                    if not (isinstance(b, int) and b == 0):
                        sp.wait_ge(L.s_ln, 4 * (u0 + u))
                    sp.wait_ge(L.s_x_in, 16 * (n_batch + b + 1))
                    load_x((b + 1) % B, (b + 1) % 2)
                if fin:
                    if not (isinstance(c, int) and c == 3):
                        sp.wait_ge(L.s_fin, 4 * (c - 3))
                    sp.dma_start(L.x1[:, :, :], x1[c - 3]).then_inc(L.s_x1_in, 16)
                if att:
                    for q in range(TC):
                        s = TC * h + q
                        sp.wait_ge(L.s_masked, u_prep + u + q + 1)
                        load_mask(b if h == 0 else (b + 1) % B, s + TC)
                if rt and not last:
                    sp.wait_ge(L.s_xo, 2 * (c0 + c - 1))
                    sp.dma_start(x_out[c - 2], L.xo[:, :, :]).then_inc(L.s_xst, 16)
                if fin:
                    sp.wait_ge(L.s_fin, 4 * (c - 2))
                    sp.dma_start(x_out[c - 3], L.xo[:, :, :]).then_inc(L.s_xst, 16)

            batches(emit, sp.Fori)
            sp.wait_ge(L.s_xst, 16 * (c0 + C))
            sp.wait_ge(L.s_x_in, 16 * (n_batch + B + 1))
            for i in range(TC):
                sp.wait_ge(L.s_mask[i], 16 * (m0 + (U + TC) // TC))

        @block.gpsimd
        def _(pool):
            if layer == 0:
                make_identity(pool, L.ident, L.s_ident)
                pool.memset(L.half[:, :], -0.5).then_inc(L.s_half, 1)
                pool.memset(L.eps[:, :], EPS).then_inc(L.s_half, 1)
                for i in range(2):
                    pool.memset(L.x_hi[:, i, :, D:D + 1].bitcast(F32), 1.0).then_inc(L.s_ones, 1)
                    pool.memset(L.x_hi[:, i, :, D + 1:DE].bitcast(F32), 0.0).then_inc(L.s_ones, 1)
                pool.wait_ge(L.s_half, 2)

            def x_lo(n, par, v):
                pool.wait_ge(L.s_x_hi, NT * (n_batch + n) + v + 1)
                pool.tensor_tensor(L.x_lo[:, par, v, :], L.x[:, par, v, :], L.x_hi[:, par, v, 0:D].bitcast(F32),
                                   ALU.subtract).then_inc(L.s_x_lo, 1)

            def add(u, i):
                pool.wait_ge(L.s_relu, u_prep + u + 1)
                pool.tensor_tensor(L.r[i][:, :], L.r[i][:, :], L.t[i][:, :], ALU.add).then_inc(L.s_sadd, 1)

            for v in range(NT):
                x_lo(0, 0, v)
            add(0, 0)
            add(1, 1)

            def emit(b, h, att, ffn, rt, fin):
                u, c = NT * b + TC * h, NCH * b + h
                for q in range(TC):
                    s = TC * h + q
                    if att:
                        if 2 <= s <= 5:
                            x_lo(b + 1, (b + 1) % 2, 2 * s - 4)
                            x_lo(b + 1, (b + 1) % 2, 2 * s - 3)
                        add(u + q + 2, q % 2)
                    if q == 0 and ffn:
                        for k in range(KD):
                            pool.wait_ge(L.s_h, 2 * (KD * (c0 + c - 1) + k + 1))
                            pool.tensor_tensor(L.h_lo[:, k, :], L.h[:, k, :], L.h_hi[:, k, :].bitcast(F32),
                                               ALU.subtract).then_inc(L.s_h_lo, 1)
                    if q == 1 and ffn:
                        for f in range(KF):
                            pool.wait_ge(L.s_g_hi, KF * (c0 + c - 1) + f + 1)
                            pool.tensor_tensor(L.g_lo[:, f, :], L.g[:, f % 2, :], L.g_hi[:, f, :].bitcast(F32),
                                               ALU.subtract).then_inc(L.s_g_lo, 1)
                    if q == 2 and rt:
                        k = c0 + c - 2
                        pool.wait_ge(L.s_ln2, 2 * TC * (k + 1))
                        pool.tensor_tensor(L.ve2[:, :], L.mv2[:, :, 1], L.eps[:, :], ALU.add).then_inc(L.s_rs2, 1)
                        pool.wait_ge(L.s_rs2, rs2(c - 2, 0) + 1)
                        pool.tensor_tensor(L.rstd2[:, :], L.ve2[:, :], L.half[:, :], ALU.pow).then_inc(L.s_rs2, 1)
                        pool.wait_ge(L.s_n2, k + 1)
                        pool.tensor_tensor(L.xo[:, :, :], L.xo[:, :, :],
                                           L.g2[:, :].unsqueeze(1).to_broadcast([P, TC, D]), ALU.mult).then_inc(L.s_xo, 1)
                        pool.wait_ge(L.s_xo, 2 * k + 1)
                        pool.tensor_tensor(L.xo[:, :, :], L.xo[:, :, :],
                                           L.be2[:, :].unsqueeze(1).to_broadcast([P, TC, D]), ALU.add).then_inc(L.s_xo, 1)
                    if q == 1 and fin:
                        pool.wait_ge(L.s_x1_in, 16 * (c - 2))
                        pool.wait_ge(L.s_xo, 2 * (c0 + c - 2))
                        pool.tensor_tensor(L.xo[:, :, :], L.xo[:, :, :], L.x1[:, :, :], ALU.add).then_inc(L.s_fin, 1)
                        pool.wait_ge(L.s_fin, 4 * (c - 3) + 3)
                        pool.tensor_tensor(L.ve2[:, :], L.mv2[:, :, 1], L.eps[:, :], ALU.add).then_inc(L.s_rs2, 1)
                        pool.wait_ge(L.s_rs2, rs2(c - 3, 1) + 1)
                        pool.tensor_tensor(L.rstd2[:, :], L.ve2[:, :], L.half[:, :], ALU.pow).then_inc(L.s_rs2, 1)
                    if att:
                        pool.wait_ge(L.s_ln, 4 * (u0 + u + q + 1))
                        i = q % 2
                        pool.tensor_tensor(L.ve[:, i:i + 1], L.mv[:, i, 1:2], L.eps[:, 0:1], ALU.add).then_inc(L.s_rs, 1)
                        pool.wait_ge(L.s_rs, 2 * (u0 + u + q) + 1)
                        pool.tensor_tensor(L.rstd[:, i:i + 1], L.ve[:, i:i + 1], L.half[:, 0:1], ALU.pow).then_inc(L.s_rs, 1)

            batches(emit, pool.Fori)

        @block.scalar
        def _(act):
            act.wait_ge(L.s_w_in, 16 * 13 * (layer + 1))
            for k in range(KD):
                act.activation(L.w1[0][:, k, :], (L.t[k])[:, :], ACT.Copy).then_inc(L.s_w_hi, 1)
            for k in range(KD):
                fs = slice(k * KF // KD, (k + 1) * KF // KD)
                act.activation(L.w2[0][:, fs, :], L.r[k][:, :].rearrange("p (f d) -> p f d", d=D), ACT.Copy)\
                   .then_inc(L.s_w_hi, 1)

            def pt_hi(u, i, first):
                if not first:
                    act.wait_ge(L.s_agg, u0 + u - 1)
                for g in range(2):
                    act.wait_ge(L.s_tr, 2 * (u_tr + u) + g + 1)
                    gs = slice(g * BANK, (g + 1) * BANK)
                    act.activation(L.pT[i][0][:, gs], L.PT[:, gs], ACT.Copy).then_inc(L.s_pt_hi, 1)

            def relu(u, s):
                i = s % 2
                act.wait_ge(L.s_masked, u_prep + u + 1)
                act.activation(L.r[i][:, :], L.t[i][:, :], ACT.Relu, bias=L.a4[:, s:s + 1], scale=4.0).then_inc(L.s_relu, 1)

            def exp(u, s):
                i = s % 2
                act.wait_ge(L.s_sadd, u_prep + u + 1)
                act.wait_ge(L.s_max_step, 2 * (u_prep + u + 1))
                act.activation(L.t[i][:, :], L.r[i][:, :], ACT.Exp, bias=L.c2[:, s % TC:s % TC + 1], scale=SLOPE)\
                   .then_inc(L.s_probs, 1)

            def sj_row(n):
                act.wait_ge(L.s_sjT, n_batch + n + 1)
                if not (isinstance(n, int) and n == 0):
                    act.wait_ge(L.s_masked, u_prep + NT * n)
                act.activation(L.sj_row[:, :], L.M[:, :], ACT.Copy).then_inc(L.s_sj_row, 1)

            sj_row(0)
            act.wait_ge(L.s_prep, n_batch * 2 + 2)
            relu(0, 0)
            relu(1, 1)
            exp(0, 0)
            exp(1, 1)
            pt_hi(0, 0, True)

            def emit(b, h, att, ffn, rt, fin):
                u, c = NT * b + TC * h, NCH * b + h
                for q in range(TC):
                    s = TC * h + q
                    if att:
                        pt_hi(u + q + 1, (q + 1) % 2, isinstance(b, int) and b == 0 and s == 0)
                    if q == 0 and ffn:
                        k0 = KD * (c0 + c - 1)
                        if not (isinstance(c, int) and c == 1):
                            act.wait_ge(L.s_res, k0)
                        for k in range(KD):
                            act.wait_ge(L.s_hT, k0 + k + 1)
                            for dst in (L.h, L.h_hi):
                                act.activation(dst[:, k, :], L.M[:, k * BANK:(k + 1) * BANK], ACT.Identity,
                                               bias=L.be1[:, k:k + 1], scale=L.g1[:, k:k + 1]).then_inc(L.s_h, 1)
                    if att:
                        if s == NT - 3:
                            sj_row(b + 1)
                        if s == NT - 2:
                            act.wait_ge(L.s_prep, 2 * (n_batch + b + 2))
                        relu(u + q + 2, (s + 2) % NT)
                    if q == 1 and ffn:
                        for f in range(KF):
                            k0 = KF * (c0 + c - 1)
                            act.wait_ge(L.s_ffn1, k0 + f + 1)
                            if f >= 2:
                                act.wait_ge(L.s_g_lo, k0 + f - 1)
                            act.activation(L.g[:, f % 2, :], L.G[f % 2][:, :], ACT.Gelu, bias=L.b1[:, f:f + 1])\
                               .then_inc(L.s_gelu, 1)
                    if att:
                        exp(u + q + 2, (s + 2) % NT)

            batches(emit, act.Fori)

        @block.vector
        def _(dve):
            for k in range(KD):
                dve.wait_ge(L.s_w_hi, 2 * KD * layer + k + 1)
                dve.tensor_tensor(L.w1[1][:, k, :], L.t[k][:, :], L.w1[0][:, k, :].bitcast(F32), ALU.subtract)\
                   .then_inc(L.s_w_lo, 1)
            for k in range(KD):
                fs = slice(k * KF // KD, (k + 1) * KF // KD)
                dve.wait_ge(L.s_w_hi, 2 * KD * layer + KD + k + 1)
                dve.tensor_tensor(L.w2[1][:, fs, :], L.r[k][:, :].rearrange("p (f d) -> p f d", d=D),
                                  L.w2[0][:, fs, :].bitcast(F32), ALU.subtract).then_inc(L.s_w_lo, 1)

            def prep_tile(n, par, v):
                if v == 0:
                    dve.wait_ge(L.s_x_in, 16 * (n_batch + n + 1))
                dve.tensor_copy(L.x_hi[:, par, v, 0:D], L.x[:, par, v, :]).then_inc(L.s_x_hi, 1)
                if v >= 2:
                    dve.wait_ge(L.s_sj, 2 * (NT * (n_batch + n) + v - 1))
                for half, dst in ((0, L.si), (1, L.sj)):
                    dve.scalar_tensor_tensor(L.prod[:, 2 * (v % 2) + half, :], L.x[:, par, v, :], 1.0,
                                             L.aw[:, half, :], ALU.mult, ALU.mult, accum_out=dst[:, v:v + 1])\
                       .then_inc(L.s_sj, 1)

            def prep_batch(n, first):
                dve.wait_ge(L.s_sj, 2 * NT * (n_batch + n + 1))
                if not first:
                    dve.wait_ge(L.s_relu, u_prep + NT * n)
                dve.tensor_scalar(L.a4[:, :], L.si[:, :], L.ab[:, :], 4.0, ALU.add, ALU.mult).then_inc(L.s_prep, 1)
                dve.tensor_scalar(L.am[:, :], L.si[:, :], L.ab[:, :], SLOPE - 1.0, ALU.add, ALU.mult).then_inc(L.s_prep, 1)

            def masked(u, s, n, k, first):
                i = s % 2
                arrived = (L.s_mask[s % TC], 16 * (m0 + k + 1))
                if first:
                    dve.wait_ge(*arrived)
                else:
                    wait_alone(dve, L.s_passed, arrived, (L.s_tr, 2 * (u_tr + u - 1)))
                dve.tensor_tensor_reduce(out=L.t[i][:, :], in0=L.sj_row[:, :], in1=L.mask[s % TC][:, :], scale=1.0,
                                         scalar=LOWEST, op0=ALU.add, op1=ALU.max, accum_out=L.mx[:, i:i + 1])\
                   .then_inc(L.s_masked, 1)
                dve.wait_ge(L.s_masked, u_prep + u + 1)
                dve.wait_ge(L.s_prep, 2 * (n_batch + n + 1))
                dve.scalar_tensor_tensor(L.mp[:, i:i + 1], L.mx[:, i:i + 1], -1.0, L.am[:, s:s + 1], ALU.mult, ALU.add)\
                   .then_inc(L.s_max_step, 1)
                dve.wait_ge(L.s_max_step, 2 * (u_prep + u) + 1)
                dve.scalar_tensor_tensor(L.c2[:, s % TC:s % TC + 1], L.mx[:, i:i + 1], -SLOPE, L.mp[:, i:i + 1], ALU.mult,
                                         ALU.min).then_inc(L.s_max_step, 1)

            def pt_lo(u, i):
                for g in range(2):
                    dve.wait_ge(L.s_pt_hi, 2 * (u_tr + u) + g + 1)
                    gs = slice(g * BANK, (g + 1) * BANK)
                    dve.tensor_tensor(L.pT[i][1][:, gs], L.PT[:, gs], L.pT[i][0][:, gs].bitcast(F32), ALU.subtract)\
                       .then_inc(L.s_pt_lo, 1)

            def norm1_stats(u, s, par):
                i = s % 2
                n = 4 * (u0 + u)
                dve.wait_ge(L.s_agg, u0 + u + 1)
                dve.reciprocal(L.rinv[:, :], L.A[:, D:D + 1]).then_inc(L.s_ln, 1)
                dve.wait_ge(L.s_ln, n + 1)
                if not (isinstance(u, int) and u < 2):
                    dve.wait_ge(L.s_n1, u0 + u - 1)
                dve.scalar_tensor_tensor(L.u[:, i, :], L.A[:, 0:D], L.rinv[:, :], L.x[:, par, s, :], ALU.mult, ALU.add)\
                   .then_inc(L.s_ln, 1)
                dve.wait_ge(L.s_ln, n + 2)
                dve.bn_stats(L.st[:, i, :], L.u[:, i, :]).then_inc(L.s_ln, 1)
                wait_alone(dve, L.s_passed, (L.s_ln, n + 3))
                dve.bn_aggr(L.mv[:, i, :], L.st[:, i, :]).then_inc(L.s_ln, 1)

            def norm1_rows(u, h, q):
                i = q % 2
                dve.wait_ge(L.s_rs, 2 * (u0 + u + 1))
                dve.tensor_scalar(L.n1[:, h, q, :], L.u[:, i, :], L.mv[:, i, 0:1], L.rstd[:, i:i + 1], ALU.subtract,
                                  ALU.mult).then_inc(L.s_n1, 1)

            for v in range(NT):
                prep_tile(0, 0, v)
            prep_batch(0, True)
            dve.wait_ge(L.s_sj_row, n_batch + 1)
            dve.wait_ge(L.s_prep, 2 * (n_batch + 1))
            dve.wait_ge(L.s_w_lo, 2 * KD * (layer + 1))
            masked(0, 0, 0, 0, True)
            masked(1, 1, 0, 0, True)
            pt_lo(0, 0)

            def emit(b, h, att, ffn, rt, fin):
                u, c = NT * b + TC * h, NCH * b + h
                first = isinstance(c, int) and c == 0
                for q in range(TC):
                    s = TC * h + q
                    if (att or q == 0 and ffn) and not (first and q == 0):
                        norm1_rows(u + q - 1, (h + 1) % 2 if q == 0 else h, (q - 1) % TC)
                    if att:
                        pt_lo(u + q + 1, (q + 1) % 2)
                        if s == NT - 2:
                            dve.wait_ge(L.s_sj_row, n_batch + b + 2)
                            prep_batch(b + 1, False)
                        v = s + 2
                        masked(u + q + 2, v % NT, b + v // NT, NCH * b + v // TC, False)
                    if q == 1 and ffn:
                        k0 = KF * (c0 + c - 1)
                        if not (isinstance(c, int) and c == 1):
                            dve.wait_ge(L.s_ffn2, KD * (c0 + c - 1))
                        for f in range(KF):
                            dve.wait_ge(L.s_gelu, k0 + f + 1)
                            dve.tensor_copy(L.g_hi[:, f, :], L.g[:, f % 2, :]).then_inc(L.s_g_hi, 1)
                    if q == 1 and fin:
                        dve.wait_ge(L.s_fin, 4 * (c - 3) + 1)
                        for t in range(TC):
                            mm = dve.bn_stats(L.st2[:, t, :], L.xo[:, t, :])
                        mm.then_inc(L.s_fin, 1)
                        wait_alone(dve, L.s_passed, (L.s_fin, 4 * (c - 3) + 2))
                        for t in range(TC):
                            mm = dve.bn_aggr(L.mv2[:, t, :], L.st2[:, t, :])
                        mm.then_inc(L.s_fin, 1)
                        dve.wait_ge(L.s_rs2, rs2(c - 3, 1) + 2)
                        for t in range(TC):
                            mm = dve.tensor_scalar(L.xo[:, t, :], L.xo[:, t, :], L.mv2[:, t, 0:1], L.rstd2[:, t:t + 1],
                                                   ALU.subtract, ALU.mult)
                        mm.then_inc(L.s_fin, 1)
                    if q == 2 and rt:
                        k = c0 + c - 2
                        dve.wait_ge(L.s_rt, k + 1)
                        for t in range(TC):
                            dve.bn_stats(L.st2[:, t, :], L.M[:, t * D:(t + 1) * D]).then_inc(L.s_ln2, 1)
                        wait_alone(dve, L.s_passed, (L.s_ln2, 2 * TC * k + TC))
                        for t in range(TC):
                            dve.bn_aggr(L.mv2[:, t, :], L.st2[:, t, :]).then_inc(L.s_ln2, 1)
                        dve.wait_ge(L.s_rs2, rs2(c - 2, 0) + 2)
                        if not (isinstance(c, int) and c == 2 and layer == 0):
                            dve.wait_ge(L.s_xst, 16 * k)
                        for t in range(TC):
                            mm = dve.tensor_scalar(L.xo[:, t, :], L.M[:, t * D:(t + 1) * D], L.mv2[:, t, 0:1],
                                                   L.rstd2[:, t:t + 1], ALU.subtract, ALU.mult)
                        mm.then_inc(L.s_n2, 1)
                    if q >= 2 and ffn:
                        k = q - 2
                        n = KD * (c0 + c - 1) + k
                        dve.wait_ge(L.s_ffn2, n + 1)
                        if not (isinstance(c, int) and c == 1):
                            dve.wait_ge(L.s_rt, c0 + c - 1)
                        dve.scalar_tensor_tensor(L.rT[:, k, :], L.Y[:, :], L.b2[:, k:k + 1], L.h[:, k, :], ALU.add,
                                                 ALU.add).then_inc(L.s_res, 1)
                    if att:
                        norm1_stats(u + q, s, b % 2)
                        if 1 <= s <= 4:
                            prep_tile(b + 1, (b + 1) % 2, 2 * s - 2)
                            prep_tile(b + 1, (b + 1) % 2, 2 * s - 1)

            batches(emit, dve.Fori)

        @block.tensor
        def _(pe):
            pe.wait_ge(L.s_ident, 2)
            pe.wait_ge(L.s_ones, 4)

            def transpose_probs(u, i, first):
                pe.wait_ge(L.s_probs, u_prep + u + 1)
                for g in range(2):
                    if not first:
                        pe.wait_ge(L.s_pt_lo, 2 * (u_tr + u) - 1 + g)
                    for q in range(TC):
                        js = slice((TC * g + q) * P, (TC * g + q + 1) * P)
                        mm = pe.transpose(L.PT[:, js], L.t[i][:, js], L.ident[:, :])
                    mm.then_inc(L.s_tr, 1)

            def aggregate(u, i, b, par, first):
                pe.wait_ge(L.s_pt_lo, 2 * (u_tr + u + 1))
                if not first:
                    pe.wait_ge(L.s_ln, 4 * (u0 + u) - 2)
                for j in range(NT):
                    js = slice(j * P, (j + 1) * P)
                    hi, lo = L.pT[i][0][:, js], L.pT[i][1][:, js]
                    pe.matmul(L.A[:, 0:DE], hi, L.x_hi[:, par, j, :], start=(j == 0), stop=False)
                    pe.matmul(L.A[:, 0:DE], lo, L.x_hi[:, par, j, :], start=False, stop=False)
                    mm = pe.matmul(L.A[:, 0:D], hi, L.x_lo[:, par, j, :], start=False, stop=(j == NT - 1))
                mm.then_inc(L.s_agg, 1)

            def sj_row(n):
                pe.wait_ge(L.s_sj, 2 * NT * (n_batch + n + 1))
                for v in range(NT):
                    mm = pe.transpose(L.M[:, v * P:(v + 1) * P], L.sj[:, v:v + 1].to_broadcast([P, P]), L.ident[:, :])
                mm.then_inc(L.s_sjT, 1)

            sj_row(0)
            pe.wait_ge(L.s_w_lo, 2 * KD * (layer + 1))
            transpose_probs(0, 0, True)

            def emit(b, h, att, ffn, rt, fin):
                u, c = NT * b + TC * h, NCH * b + h
                start = isinstance(c, int) and c == 0
                for q in range(TC):
                    s = TC * h + q
                    if att:
                        transpose_probs(u + q + 1, (q + 1) % 2, False)
                        if s == 0:
                            pe.wait_ge(L.s_x_lo, NT * (n_batch + b + 1))
                        aggregate(u + q, q % 2, b, b % 2, start and q == 0)
                    if q == 0 and ffn:
                        k0 = c0 + c - 1
                        pe.wait_ge(L.s_n1, TC * (k0 + 1))
                        if isinstance(c, int) and c <= 2:
                            pe.wait_ge(L.s_sj_row, n_batch + c)
                        else:
                            pe.wait_ge(L.s_n2, k0 - 1)
                        for k in range(KD):
                            for t in range(TC):
                                mm = pe.transpose(L.M[:, k * BANK + t * P:k * BANK + (t + 1) * P],
                                                  L.n1[:, (h + 1) % 2, t, k * P:(k + 1) * P], L.ident[:, :])
                            mm.then_inc(L.s_hT, 1)
                    if att and s == NT - 3:
                        if ffn:
                            pe.wait_ge(L.s_h, 2 * KD * (c0 + c))
                        sj_row(b + 1)
                    if q == 1 and ffn:
                        k0 = c0 + c - 1
                        pe.wait_ge(L.s_h_lo, KD * (k0 + 1))
                        for f in range(KF):
                            n = KF * k0 + f
                            if not (isinstance(c, int) and c == 1 and f < 2 and layer == 0):
                                pe.wait_ge(L.s_gelu, n - 1)
                            fs = slice(f * P, (f + 1) * P)
                            for k in range(KD):
                                mm = split_product(pe, L.G[f % 2][:, :], (L.w1[0][:, k, fs], L.w1[1][:, k, fs]),
                                                   (L.h_hi[:, k, :], L.h_lo[:, k, :]), k == 0, k == KD - 1)
                            mm.then_inc(L.s_ffn1, 1)
                    if q == 1 and rt:
                        k0 = c0 + c - 2
                        if att and h == 1:
                            pe.wait_ge(L.s_sj_row, n_batch + b + 2)
                        elif ffn:
                            pe.wait_ge(L.s_h, 2 * KD * (k0 + 2))
                        else:
                            pe.wait_ge(L.s_n2, k0)
                        pe.wait_ge(L.s_res, KD * (k0 + 1))
                        for t in range(TC):
                            for k in range(KD):
                                mm = pe.transpose(L.M[:, t * D + k * P:t * D + (k + 1) * P],
                                                  L.rT[:, k, t * P:(t + 1) * P], L.ident[:, :])
                        mm.then_inc(L.s_rt, 1)
                    if q >= 2 and ffn:
                        k0 = c0 + c - 1
                        o = q - 2
                        pe.wait_ge(L.s_g_lo, KF * (k0 + 1))
                        if not (isinstance(c, int) and c == 1 and o == 0):
                            pe.wait_ge(L.s_res, KD * k0 + o)
                        os = slice(o * P, (o + 1) * P)
                        for f in range(KF):
                            mm = split_product(pe, L.Y[:, :], (L.w2[0][:, f, os], L.w2[1][:, f, os]),
                                               (L.g_hi[:, f, :], L.g_lo[:, f, :]), f == 0, f == KF - 1)
                        mm.then_inc(L.s_ffn2, 1)

            batches(emit, pe.Fori)


def program(nc, x, adj, L0_W, L0_b, L0_attn, attn_w, attn_b, W1, b1, W2, b2, g1, beta1, g2, beta2, out):
    B, N, D, _, NT, _, _ = shapes(x, W1)
    TC = BANK // P
    C = B * N // BANK
    rows = [nc.dram_tensor(f"rows{i}", (C * TC, P, D), F32, kind="Internal").ap() for i in range(3)]
    mask = nc.dram_tensor("mask", (B * NT, P, N), BF16, kind="Internal").ap()
    chunks = [r.rearrange("(c t) p d -> c p t d", t=TC) for r in rows]
    chunks.append(out.rearrange("b (c t p) d -> (b c) p t d", t=TC, p=P))
    first_stage(nc, x, adj, L0_W, L0_b, L0_attn, rows[0], mask, W1)
    par = (attn_w, attn_b, W1, b1, W2, b2, g1, beta1, g2, beta2)
    layers = W1.shape[0]
    with ExitStack() as ctx:
        L = layer_buffers(nc, ctx, x, W1)
        for layer in range(layers):
            graph_layer(nc, L, layer, x, chunks[layer], chunks[layer + 1], chunks[0], mask, par, layer == layers - 1)


_INS = ['x', 'adj', 'L0_gnn_W', 'L0_gnn_b', 'L0_gnn_attn', 'L1_gnn_attn_w', 'L1_gnn_attn_b', 'L1_gnn_W1', 'L1_gnn_b1',
        'L1_gnn_W2', 'L1_gnn_b2', 'L1_gnn_g1', 'L1_gnn_beta1', 'L1_gnn_g2', 'L1_gnn_beta2']


def kernel(**inputs):
    import numpy as _np
    import concourse.bacc as _bacc
    from concourse import mybir as _mybir
    from concourse.bass_utils import run_bass_kernel_spmd as _run

    nc = _bacc.Bacc("TRN2", target_bir_lowering=False, num_devices=1)
    arrays, args = {}, []
    for name in _INS:
        a = _np.ascontiguousarray(inputs[name])
        arrays[f"in_{name}"] = a
        args.append(nc.dram_tensor(f"in_{name}", a.shape, _mybir.dt.from_np(a.dtype), kind="ExternalInput").ap())
    shape = inputs["x"].shape
    args.append(nc.dram_tensor("out_rows", shape, _mybir.dt.float32, kind="ExternalOutput").ap())
    program(nc, *args)
    r = _run(nc, [arrays], core_ids=[0])
    return r.results[0]["out_rows"]
```

```python
from contextlib import ExitStack

import concourse.bass as bass
from concourse import mybir


P = 128
F32 = mybir.dt.float32
F32R = mybir.dt.float32r
BF16 = mybir.dt.bfloat16
I32 = mybir.dt.int32
ALU = mybir.AluOpType
ACT = mybir.ActivationFunctionType

MASKED = -1.0e30
LOWEST = -3.0e38
EPS = 1e-5
SLOPE = 0.2
BANK = 512
AHEAD = 3
G_RING = 3


def shapes(x, w1):
    B, N, D = x.shape
    F = w1.shape[2]
    return B, N, D, F, N // P, D // P, F // P


def split_product(pe, out, hi_lo_left, hi_lo_right, start, stop):
    (left_hi, left_lo), (right_hi, right_lo) = hi_lo_left, hi_lo_right
    pe.matmul(out, left_hi, right_hi, start=start, stop=False)
    pe.matmul(out, left_lo, right_hi, start=False, stop=False)
    return pe.matmul(out, left_hi, right_lo, start=False, stop=stop)


def wait_alone(eng, passed, *waits):
    for sem, value in waits:
        eng.wait_ge(sem, value)
    eng.sem_inc(passed, 1)


def make_identity(pool, ident, done):
    pool.memset(ident[:, :], 0.0).then_inc(done, 1)
    pool.wait_ge(done, 1)
    pool.affine_select(out=ident[:, :], in_=ident[:, :], compare_op=ALU.not_equal, fill=1.0,
                       base=0, pattern=[[-1, P]], channel_multiplier=1).then_inc(done, 1)


def first_stage(nc, x, adj, W, bias, attn, x1_dram, mask_dram, w1):
    B, N, D, _, NT, KD, _ = shapes(x, w1)
    NC = N // BANK
    TC = BANK // P
    DE = D + 2
    AR = 4
    PJ = 4 * NC * KD
    with ExitStack() as ctx:
        def sb(name, shape, dt=F32):
            return ctx.enter_context(nc.sbuf_tensor("a_" + name, shape, dt))

        def sem(name):
            return ctx.enter_context(nc.semaphore("a_" + name))

        ident = sb("ident", [P, P])
        ident_r = sb("ident_r", [P, P], F32R)
        w_in = sb("w_in", [P, KD, D])
        at_in = sb("at_in", [P, KD, D])
        bias_col = sb("bias_col", [P, KD])
        wT = [sb("wT_hi", [P, KD, D], F32R), sb("wT_lo", [P, KD, D], F32R)]
        at = [sb("at_hi", [P, KD, D], F32R), sb("at_lo", [P, KD, D], F32R)]
        xs = sb("xs", [P, NT, D])
        xr = sb("xr", [P, NT, D])
        xT = [sb("xT_hi", [P, KD, N], F32R), sb("xT_lo", [P, KD, N], F32R)]
        hT = [sb("hT_hi", [P, KD, N], F32R), sb("hT_lo", [P, KD, N], F32R)]
        haT = [sb("haT_hi", [P, KD, N], F32R), sb("haT_lo", [P, KD, N], F32R)]
        hn = [sb("hn_hi", [P, NT, DE], F32R), sb("hn_lo", [P, NT, D], F32R)]
        adj_t = sb("adj_t", [P, AR, N], I32)
        mask0 = sb("mask0", [P, 2, N], BF16)
        mask1 = sb("mask1", [P, 2, N], BF16)
        t = [sb(f"t{i}", [P, N]) for i in range(2)]
        pT = [[sb(f"pT_hi{i}", [P, N], F32R), sb(f"pT_lo{i}", [P, N], F32R)] for i in range(2)]
        mx = sb("mx", [P, 2])
        nmx = sb("nmx", [P, 2])
        rinv = sb("rinv", [P, 1])
        neg = sb("neg", [P, 2, D])
        y = sb("y", [P, 2, D])
        stats = sb("stats", [P, 2, 6])
        mv = sb("mv", [P, 2, 2])
        ve = sb("ve", [P, 2])
        rstd = sb("rstd", [P, 2])
        half = sb("half", [P, 1])
        eps = sb("eps", [P, 1])
        xo = sb("xo", [P, 2, D])

        S = [ctx.enter_context(nc.psum_tensor(f"a_S{i}", [P, N], F32)) for i in range(2)]
        PT = ctx.enter_context(nc.psum_tensor("a_PT", [P, N], F32))
        O = [ctx.enter_context(nc.psum_tensor(f"a_O{i}", [P, BANK], F32)) for i in range(2)]
        pj_bank = [S[0][:, 0:BANK], S[0][:, BANK:N]]

        s_id = sem("ident")
        s_idr = sem("ident_r")
        s_half = sem("half")
        s_ones = sem("ones")
        s_w = sem("weights_in")
        s_wt = sem("w_transposed")
        s_whi = sem("weights_hi")
        s_wlo = sem("weights_lo")
        s_xs = sem("xs_in")
        s_xr = sem("xr_in")
        s_adj = [sem(f"adj_in{i}") for i in range(AR)]
        s_mask = sem("mask_step")
        s_mst = [sem(f"mask_stored{i}") for i in range(2)]
        s_mm = sem("proj_product")
        s_phi = sem("proj_hi")
        s_plo = sem("proj_lo")
        s_s = sem("scores")
        s_t = sem("masked")
        s_nm = sem("max_negated")
        s_p = sem("probs")
        s_tr = sem("probs_transposed")
        s_thi = sem("probsT_hi")
        s_tlo = sem("probsT_lo")
        s_pv = sem("values")
        s_ln = sem("norm_step")
        s_ex = sem("elu_exp")
        s_passed = sem("passed")
        s_rs = sem("rstd_step")
        s_st = [sem(f"x1_stored{i}") for i in range(2)]
        LN = 8

        block = ctx.enter_context(nc.Block())

        @block.sync
        def _(sp):
            sp.dma_start(w_in[:, :, :], W.rearrange("(k p) i -> p k i", p=P)).then_inc(s_w, 16)
            sp.dma_start(at_in[:, :, :], attn.rearrange("(k p) j -> p k j", p=P)).then_inc(s_w, 16)
            with nc.allow_non_contiguous_dma("a column of the bias"):
                sp.dma_start(bias_col[:, :], bias.rearrange("(k p) -> p k", p=P)).then_inc(s_w, 16)
            sp.dma_start(xs[:, :, :], x[0].rearrange("(t p) d -> p t d", p=P)).then_inc(s_xs, 16)

            def batch(b, first):
                for k in range(NT):
                    if not (first and k < AR):
                        sp.wait_ge(s_mask, 3 * (NT * b + k - AR + 1))
                    sp.dma_start(adj_t[:, k % AR, :], adj[b, k * P:(k + 1) * P, :]).then_inc(s_adj[k % AR], 16)
                    if k == 1:
                        if not first:
                            sp.wait_ge(s_ln, LN * (NT * b - 1) + 4)
                        sp.dma_start(xr[:, :, :], x[b].rearrange("(t p) d -> p t d", p=P)).then_inc(s_xr, 16)
                    if k == 3:
                        sp.wait_ge(s_mm, PJ * b + NC * KD)
                        sp.dma_start(xs[:, :, :], x[(b + 1) % B].rearrange("(t p) d -> p t d", p=P)).then_inc(s_xs, 16)
                    if k >= 3:
                        store_mask(b, k - 3)
                    if k >= 5:
                        store_x1(b, k - 5)
                for k in range(NT - 3, NT):
                    store_mask(b, k)
                    store_x1(b, k - 2)
                for k in range(NT - 2, NT):
                    store_x1(b, k)

            def store_mask(b, k):
                sp.wait_ge(s_mask, 3 * (NT * b + k + 1))
                sp.dma_start(mask_dram[b * NT + k], mask1[:, k % 2, :]).then_inc(s_mst[k % 2], 16)

            def store_x1(b, k):
                sp.wait_ge(s_ln, LN * (NT * b + k + 1))
                sp.dma_start(x1_dram[b * NT + k], xo[:, k % 2, :]).then_inc(s_st[k % 2], 16)

            batch(0, True)
            with sp.Fori(1, B) as b:
                batch(b, False)
            for i in range(2):
                sp.wait_ge(s_mst[i], 16 * B * NT // 2)
                sp.wait_ge(s_st[i], 16 * B * NT // 2)
            sp.wait_ge(s_xs, 16 * (B + 1))

        @block.gpsimd
        def _(pool):
            make_identity(pool, ident, s_id)
            pool.memset(half[:, :], -0.5).then_inc(s_half, 1)
            pool.memset(eps[:, :], EPS).then_inc(s_half, 1)
            pool.memset(hn[0][:, :, D:D + 1].bitcast(F32), 1.0).then_inc(s_ones, 1)
            pool.memset(hn[0][:, :, D + 1:DE].bitcast(F32), 0.0).then_inc(s_ones, 1)
            pool.wait_ge(s_half, 2)

            def batch(b):
                for k in range(NT):
                    n = NT * b + k
                    i = k % 2
                    pool.wait_ge(s_ln, LN * n + 7)
                    pool.tensor_tensor(ve[:, i:i + 1], mv[:, i, 1:2], eps[:, :], ALU.add).then_inc(s_rs, 1)
                    pool.wait_ge(s_rs, 2 * n + 1)
                    pool.tensor_tensor(rstd[:, i:i + 1], ve[:, i:i + 1], half[:, :], ALU.pow).then_inc(s_rs, 1)

            with pool.Fori(0, B) as b:
                batch(b)

        @block.scalar
        def _(act):
            act.wait_ge(s_w, 48)
            act.activation(at[0][:, :, :], at_in[:, :, :], ACT.Copy).then_inc(s_whi, 1)
            act.wait_ge(s_wt, KD * KD)
            for k in range(KD):
                act.activation(wT[0][:, k, :], PT[:, k * BANK:k * BANK + D], ACT.Copy).then_inc(s_whi, 1)

            def proj_hi(b, p):
                part, c, k = p // (NC * KD), p % (NC * KD) // KD, p % KD
                act.wait_ge(s_mm, PJ * b + p + 1)
                src = pj_bank[p % 2]
                cs = slice(c * BANK, (c + 1) * BANK)
                if part == 0:
                    act.activation(xT[0][:, k, cs], src, ACT.Copy).then_inc(s_phi, 1)
                elif part == 1:
                    act.activation(hT[0][:, k, cs], src, ACT.Identity, bias=bias_col[:, k:k + 1]).then_inc(s_phi, 1)
                elif part == 2:
                    act.activation(haT[0][:, k, cs], src, ACT.Copy).then_inc(s_phi, 1)
                else:
                    g = p % (NC * KD)
                    act.activation(hn[0][:, 2 * g:2 * g + 2, 0:D], src.rearrange("p (t d) -> p t d", d=D),
                                   ACT.Copy).then_inc(s_phi, 1)

            def softmax_exp(b, k):
                act.wait_ge(s_nm, NT * b + k + 1)
                act.activation(t[k % 2][:, :], t[k % 2][:, :], ACT.Exp, bias=nmx[:, k % 2:k % 2 + 1]).then_inc(s_p, 1)

            def transposed_hi(b, k, first):
                if not (first and k < 2):
                    act.wait_ge(s_pv, NT * b + k - 1)
                for g in range(2):
                    act.wait_ge(s_tr, 2 * (NT * b + k) + g + 1)
                    gs = slice(g * BANK, (g + 1) * BANK)
                    act.activation(pT[k % 2][0][:, gs], PT[:, gs], ACT.Copy).then_inc(s_thi, 1)

            def batch(b, first):
                for p in range(PJ):
                    proj_hi(b, p)
                softmax_exp(b, 0)
                softmax_exp(b, 1)
                transposed_hi(b, 0, first)
                for k in range(NT):
                    if k + 1 < NT:
                        transposed_hi(b, k + 1, first)
                    if k + 2 < NT:
                        softmax_exp(b, k + 2)
                    act.wait_ge(s_ln, LN * (NT * b + k) + 3)
                    act.activation(neg[:, k % 2, :], neg[:, k % 2, :], ACT.Exp).then_inc(s_ex, 1)

            batch(0, True)
            with act.Fori(1, B) as b:
                batch(b, False)

        @block.vector
        def _(dve):
            dve.wait_ge(s_id, 2)
            dve.tensor_copy(ident_r[:, :], ident[:, :]).then_inc(s_idr, 1)
            dve.wait_ge(s_whi, 1)
            dve.tensor_tensor(at[1][:, :, :], at_in[:, :, :], at[0][:, :, :].bitcast(F32), ALU.subtract).then_inc(s_wlo, 1)
            for k in range(KD):
                dve.wait_ge(s_whi, 2 + k)
                dve.tensor_tensor(wT[1][:, k, :], PT[:, k * BANK:k * BANK + D], wT[0][:, k, :].bitcast(F32),
                                  ALU.subtract).then_inc(s_wlo, 1)

            def proj_lo(b, p):
                part, c, k = p // (NC * KD), p % (NC * KD) // KD, p % KD
                dve.wait_ge(s_phi, PJ * b + p + 1)
                src = pj_bank[p % 2]
                cs = slice(c * BANK, (c + 1) * BANK)
                if part == 0:
                    dve.tensor_tensor(xT[1][:, k, cs], src, xT[0][:, k, cs].bitcast(F32), ALU.subtract).then_inc(s_plo, 1)
                elif part == 1:
                    dve.scalar_tensor_tensor(hT[1][:, k, cs], src, bias_col[:, k:k + 1], hT[0][:, k, cs].bitcast(F32),
                                             ALU.add, ALU.subtract).then_inc(s_plo, 1)
                elif part == 2:
                    dve.tensor_tensor(haT[1][:, k, cs], src, haT[0][:, k, cs].bitcast(F32), ALU.subtract).then_inc(s_plo, 1)
                else:
                    g = p % (NC * KD)
                    dve.tensor_tensor(hn[1][:, 2 * g:2 * g + 2, :], src.rearrange("p (t d) -> p t d", d=D),
                                      hn[0][:, 2 * g:2 * g + 2, 0:D].bitcast(F32), ALU.subtract).then_inc(s_plo, 1)

            def masks(b, k, first):
                n = NT * b + k
                i, a = k % 2, k % AR
                dve.wait_ge(s_adj[a], 16 * (NT // AR * b + k // AR + 1))
                dve.tensor_scalar(mask0[:, i, :], adj_t[:, a, :], 0.0, MASKED, ALU.is_equal, ALU.mult).then_inc(s_mask, 1)
                dve.wait_ge(s_mask, 3 * n + 1)
                dg = adj_t[:, a, k * P:(k + 1) * P]
                dve.tensor_tensor(dg, dg, ident[:, :], ALU.add).then_inc(s_mask, 1)
                dve.wait_ge(s_mask, 3 * n + 2)
                if not (first and k < 2):
                    dve.wait_ge(s_mst[i], 16 * (NT // 2 * b + k // 2))
                dve.tensor_scalar(mask1[:, i, :], adj_t[:, a, :], 0.0, MASKED, ALU.is_le, ALU.mult).then_inc(s_mask, 1)

            def masked_scores(b, k, first):
                n = NT * b + k
                i = k % 2
                if first and k < 2:
                    dve.wait_ge(s_s, n + 1)
                else:
                    wait_alone(dve, s_passed, (s_s, n + 1), (s_tr, 2 * (n - 1)))
                dve.tensor_tensor_reduce(out=t[i][:, :], in0=S[i][:, :], in1=mask0[:, i, :], scale=1.0, scalar=LOWEST,
                                         op0=ALU.add, op1=ALU.max, accum_out=mx[:, i:i + 1]).then_inc(s_t, 1)
                dve.wait_ge(s_t, n + 1)
                dve.tensor_scalar(nmx[:, i:i + 1], mx[:, i:i + 1], -1.0, None, ALU.mult).then_inc(s_nm, 1)

            def transposed_lo(b, k):
                for g in range(2):
                    dve.wait_ge(s_thi, 2 * (NT * b + k) + g + 1)
                    gs = slice(g * BANK, (g + 1) * BANK)
                    dve.tensor_tensor(pT[k % 2][1][:, gs], PT[:, gs], pT[k % 2][0][:, gs].bitcast(F32),
                                      ALU.subtract).then_inc(s_tlo, 1)

            def elu_norm(b, k, first):
                n = NT * b + k
                i = k % 2
                o = O[i][:, 0:D]
                dve.wait_ge(s_pv, n + 1)
                dve.reciprocal(rinv[:, :], O[i][:, D:D + 1]).then_inc(s_ln, 1)
                dve.wait_ge(s_ln, LN * n + 1)
                dve.tensor_scalar(y[:, i, :], o, rinv[:, :], 0.0, ALU.mult, ALU.max).then_inc(s_ln, 1)
                dve.tensor_scalar(neg[:, i, :], o, rinv[:, :], 0.0, ALU.mult, ALU.min).then_inc(s_ln, 1)
                if k == 0:
                    dve.wait_ge(s_xr, 16 * (b + 1))
                dve.wait_ge(s_ln, LN * n + 2)
                dve.scalar_tensor_tensor(y[:, i, :], y[:, i, :], -1.0, xr[:, k, :], ALU.add, ALU.add).then_inc(s_ln, 1)

            def elu_norm2(b, k, first):
                n = NT * b + k
                i = k % 2
                dve.wait_ge(s_ln, LN * n + 4)
                dve.wait_ge(s_ex, n + 1)
                dve.tensor_tensor(y[:, i, :], y[:, i, :], neg[:, i, :], ALU.add).then_inc(s_ln, 1)
                dve.wait_ge(s_ln, LN * n + 5)
                dve.bn_stats(stats[:, i, :], y[:, i, :]).then_inc(s_ln, 1)
                wait_alone(dve, s_passed, (s_ln, LN * n + 6))
                dve.bn_aggr(mv[:, i, :], stats[:, i, :]).then_inc(s_ln, 1)
                dve.wait_ge(s_rs, 2 * n + 2)
                if not (first and k < 2):
                    dve.wait_ge(s_st[i], 16 * (NT // 2 * b + k // 2))
                dve.tensor_scalar(xo[:, i, :], y[:, i, :], mv[:, i, 0:1], rstd[:, i:i + 1], ALU.subtract,
                                  ALU.mult).then_inc(s_ln, 1)

            def batch(b, first):
                masks(b, 0, first)
                for p in range(PJ):
                    proj_lo(b, p)
                masks(b, 1, first)
                masked_scores(b, 0, first)
                masked_scores(b, 1, first)
                masks(b, 2, first)
                transposed_lo(b, 0)
                for k in range(NT):
                    if k + 1 < NT:
                        transposed_lo(b, k + 1)
                    if k + 2 < NT:
                        masked_scores(b, k + 2, first)
                    elu_norm(b, k, first)
                    if k + 3 < NT:
                        masks(b, k + 3, first)
                    elu_norm2(b, k, first)

            batch(0, True)
            with dve.Fori(1, B) as b:
                batch(b, False)

        @block.tensor
        def _(pe):
            pe.wait_ge(s_id, 2)
            pe.wait_ge(s_w, 48)
            for k in range(KD):
                for o in range(KD):
                    pe.transpose(PT[:, k * BANK + o * P:k * BANK + (o + 1) * P], w_in[:, o, k * P:(k + 1) * P],
                                 ident[:, :]).then_inc(s_wt, 1)
            pe.wait_ge(s_idr, 1)
            pe.wait_ge(s_wlo, 1 + KD)
            pe.wait_ge(s_ones, 2)

            def bank_free(b, p, first):
                if p >= 2:
                    pe.wait_ge(s_plo, PJ * b + p - 1)
                elif not first:
                    pe.wait_ge(s_t, NT * b)

            def projections(b, first):
                pe.wait_ge(s_xs, 16 * (b + 1))
                p = 0
                for c in range(NC):
                    for k in range(KD):
                        bank_free(b, p, first)
                        for q in range(TC):
                            mm = pe.transpose(pj_bank[p % 2][:, q * P:(q + 1) * P],
                                              xs[:, TC * c + q, k * P:(k + 1) * P], ident[:, :])
                        mm.then_inc(s_mm, 1)
                        p += 1
                for src, w, parts in ((xT, wT, 0), (hT, at, 1)):
                    for c in range(NC):
                        cs = slice(c * BANK, (c + 1) * BANK)
                        pe.wait_ge(s_plo, PJ * b + NC * KD * parts + KD * (c + 1))
                        for o in range(KD):
                            bank_free(b, p, first)
                            os = slice(o * P, (o + 1) * P)
                            for k in range(KD):
                                mm = split_product(pe, pj_bank[p % 2], (w[0][:, k, os], w[1][:, k, os]),
                                                   (src[0][:, k, cs], src[1][:, k, cs]), k == 0, k == KD - 1)
                            mm.then_inc(s_mm, 1)
                            p += 1
                for g in range(NT // 2):
                    bank_free(b, p, first)
                    for q in range(2):
                        ts = slice((2 * g + q) * P, (2 * g + q + 1) * P)
                        for k in range(KD):
                            out = pj_bank[p % 2][:, q * D + k * P:q * D + (k + 1) * P]
                            pe.matmul(out, hT[0][:, k, ts], ident_r[:, :], start=True, stop=False)
                            mm = pe.matmul(out, hT[1][:, k, ts], ident_r[:, :], start=False, stop=True)
                    mm.then_inc(s_mm, 1)
                    p += 1
                assert p == PJ

            def scores(b, j, first):
                n = NT * b + j
                if j >= 2:
                    pe.wait_ge(s_t, n - 1)
                elif j == 1 and not first:
                    pe.wait_ge(s_t, n - 1)
                ts = slice(j * P, (j + 1) * P)
                for c in range(NC):
                    cs = slice(c * BANK, (c + 1) * BANK)
                    for k in range(KD):
                        mm = split_product(pe, S[j % 2][:, cs], (haT[0][:, k, ts], haT[1][:, k, ts]),
                                           (hT[0][:, k, cs], hT[1][:, k, cs]), k == 0, k == KD - 1)
                mm.then_inc(s_s, 1)

            def transpose_probs(b, j, first):
                n = NT * b + j
                pe.wait_ge(s_p, n + 1)
                for g in range(2):
                    if not (first and j == 0):
                        pe.wait_ge(s_tlo, 2 * n - 1 + g)
                    for q in range(TC):
                        js = slice((TC * g + q) * P, (TC * g + q + 1) * P)
                        mm = pe.transpose(PT[:, js], t[j % 2][:, js], ident[:, :])
                    mm.then_inc(s_tr, 1)

            def values(b, k, first):
                n = NT * b + k
                pe.wait_ge(s_tlo, 2 * n + 2)
                if not (first and k < 2):
                    pe.wait_ge(s_ln, LN * (n - 2) + 3)
                for j in range(NT):
                    js = slice(j * P, (j + 1) * P)
                    pe.matmul(O[k % 2][:, 0:DE], pT[k % 2][0][:, js], hn[0][:, j, :], start=(j == 0), stop=False)
                    pe.matmul(O[k % 2][:, 0:DE], pT[k % 2][1][:, js], hn[0][:, j, :], start=False, stop=False)
                    mm = pe.matmul(O[k % 2][:, 0:D], pT[k % 2][0][:, js], hn[1][:, j, :], start=False, stop=(j == NT - 1))
                mm.then_inc(s_pv, 1)

            def batch(b, first):
                projections(b, first)
                pe.wait_ge(s_plo, PJ * (b + 1))
                scores(b, 0, first)
                scores(b, 1, first)
                transpose_probs(b, 0, first)
                for k in range(NT):
                    if k + 2 < NT:
                        scores(b, k + 2, first)
                    if k + 1 < NT:
                        transpose_probs(b, k + 1, first)
                    values(b, k, first)

            batch(0, True)
            with pe.Fori(1, B) as b:
                batch(b, False)


class Layers:
    pass


def layer_buffers(nc, ctx, x, w1):
    B, N, D, F, NT, KD, KF = shapes(x, w1)
    L = Layers()

    def sb(name, shape, dt=F32):
        return ctx.enter_context(nc.sbuf_tensor(name, shape, dt))

    def ps(name, cols):
        return ctx.enter_context(nc.psum_tensor(name, [P, cols], F32))

    def sem(name):
        return ctx.enter_context(nc.semaphore(name))

    DE = D + 2
    TC = BANK // P
    L.ident = sb("ident", [P, P])
    L.half = sb("half", [P, TC])
    L.eps = sb("eps", [P, TC])
    L.w1 = [sb("w1_hi", [P, KD, F], F32R), sb("w1_lo", [P, KD, F], F32R)]
    L.w2 = [sb("w2_hi", [P, KF, D], F32R), sb("w2_lo", [P, KF, D], F32R)]
    L.b1 = sb("b1", [P, KF])
    L.b2 = sb("b2", [P, KD])
    L.g1 = sb("g1", [P, KD])
    L.be1 = sb("be1", [P, KD])
    L.g2 = sb("g2", [P, D])
    L.be2 = sb("be2", [P, D])
    L.aw = sb("aw", [P, 2, D])
    L.ab = sb("ab", [P, 1])
    L.mask = [sb(f"mask{i}", [P, N], BF16) for i in range(TC)]
    L.x = sb("x", [P, 2, NT, D])
    L.x_hi = sb("x_hi", [P, 2, NT, DE], F32R)
    L.x_lo = sb("x_lo", [P, 2, NT, D], F32R)
    L.prod = sb("prod", [P, 2, D])
    L.si = sb("si", [P, NT])
    L.sj = sb("sj", [P, NT])
    L.a8 = sb("a8", [P, NT])
    L.sj_row = sb("sj_row", [P, 2, N])
    L.t = [sb(f"t{i}", [P, N]) for i in range(TC)]
    L.mx = sb("mx", [P, TC])
    L.nmx = sb("nmx", [P, TC])
    L.pT = [[sb(f"pT_hi{i}", [P, N], F32R), sb(f"pT_lo{i}", [P, N], F32R)] for i in range(2)]
    L.rinv = sb("rinv", [P, 1])
    L.u = sb("u", [P, 2, D])
    L.st = sb("st", [P, 2, 6])
    L.mv = sb("mv", [P, 2, 2])
    L.ve = sb("ve", [P, 2])
    L.rstd = sb("rstd", [P, 2])
    L.n1 = sb("n1", [P, 2, TC, D])
    L.h = sb("h", [P, KD, BANK])
    L.h_hi = sb("h_hi", [P, KD, BANK], F32R)
    L.h_lo = sb("h_lo", [P, KD, BANK], F32R)
    L.g = sb("g", [P, G_RING, BANK])
    L.g_hi = sb("g_hi", [P, KF, BANK], F32R)
    L.g_lo = sb("g_lo", [P, KF, BANK], F32R)
    L.rT = sb("rT", [P, KD, BANK])
    L.st2 = sb("st2", [P, TC, 6])
    L.mv2 = sb("mv2", [P, TC, 2])
    L.ve2 = sb("ve2", [P, TC])
    L.rstd2 = sb("rstd2", [P, TC])
    L.xo = sb("xo", [P, TC, D])
    L.x1 = sb("x1", [P, TC, D])

    L.PT = ps("PT", N)
    L.A = ps("A", BANK)
    L.G = [ps(f"G{i}", BANK) for i in range(2)]
    L.Y = ps("Y", BANK)
    L.M = ps("M", 2 * BANK)

    L.s_ident = sem("ident")
    L.s_half = sem("half")
    L.s_ones = sem("ones")
    L.s_w_in = sem("w_in")
    L.s_w_hi = sem("w_hi")
    L.s_w_lo = sem("w_lo")
    L.s_x_in = sem("x_in")
    L.s_x_hi = sem("x_hi")
    L.s_x_lo = sem("x_lo")
    L.s_sj = sem("sj")
    L.s_prep = sem("prep")
    L.s_sjT = sem("sjT")
    L.s_sj_row = sem("sj_row")
    L.s_score = sem("score")
    L.s_masked = sem("masked")
    L.s_nmx = sem("nmx")
    L.s_probs = sem("probs")
    L.s_tr = sem("tr")
    L.s_pt_hi = sem("pt_hi")
    L.s_pt_lo = sem("pt_lo")
    L.s_agg = sem("agg")
    L.s_ln = sem("ln")
    L.s_rs = sem("rs")
    L.s_n1 = sem("n1")
    L.s_hT = sem("hT")
    L.s_h = sem("h")
    L.s_h_lo = sem("h_lo")
    L.s_ffn1 = sem("ffn1")
    L.s_gelu = sem("gelu")
    L.s_g_lo = sem("g_lo")
    L.s_ffn2 = sem("ffn2")
    L.s_res = sem("res")
    L.s_rt = sem("rt")
    L.s_ln2 = sem("ln2")
    L.s_rs2 = sem("rs2")
    L.s_n2 = sem("n2")
    L.s_xo = sem("xo")
    L.s_xst = sem("xst")
    L.s_x1_in = sem("x1_in")
    L.s_fin = sem("fin")
    L.s_passed = sem("passed")
    L.s_mask = [sem(f"mask_in{i}") for i in range(TC)]
    return L


def graph_layer(nc, L, layer, x, x_in, x_out, x1, mask, par, last):
    aw, ab, W1, b1, W2, b2, g1, be1, g2, be2 = par
    B, N, D, F, NT, KD, KF = shapes(x, W1)
    DE, TC = D + 2, BANK // P
    NCH = N // BANK
    C = B * NCH
    U = B * NT
    assert NCH == 2 and NT == NCH * TC and KF == NT
    u_prep, u_exp, u_tr, n_batch = layer * (U + AHEAD), layer * (U + AHEAD - 1), layer * (U + 1), layer * (B + 1)
    lo_beside = {2: range(NT // 2), 3: range(NT // 2, NT)}
    u0, c0, m0 = layer * U, layer * C, layer * (U + TC) // TC

    def rs2(c, final):
        return 2 * c0 + (4 * c + 2 * final if last else 2 * c)

    def batches(emit, loop):
        for b in range(2):
            for h in range(NCH):
                c = NCH * b + h
                emit(b, h, True, c >= 1, c >= 2, c >= 3)
        with loop(2, B) as b:
            for h in range(NCH):
                emit(b, h, True, True, True, True)
        emit(B, 0, False, True, True, True)
        emit(B, 1, False, False, True, True)
        emit(B + 1, 0, False, False, False, True)

    with nc.Block() as block:
        @block.sync
        def _(sp):
            stage = L.t
            for k in range(KD):
                sp.dma_start(stage[k][:, :], W1[layer, k * P:(k + 1) * P, :]).then_inc(L.s_w_in, 16)
            w2 = W2[layer].rearrange("(f p) d -> p f d", p=P)
            for k in range(KD):
                fs = slice(k * KF // KD, (k + 1) * KF // KD)
                sp.dma_start(stage[KD + k][:, :].rearrange("p (f d) -> p f d", d=D), w2[:, fs, :]).then_inc(L.s_w_in, 16)
            with nc.allow_non_contiguous_dma("columns of the layer's vectors"):
                for dst, src in ((L.b1, b1), (L.b2, b2), (L.g1, g1), (L.be1, be1)):
                    sp.dma_start(dst[:, :], src[layer].rearrange("(k p) -> p k", p=P)).then_inc(L.s_w_in, 16)
                for dst, src in ((L.g2[:, :], g2[layer]), (L.be2[:, :], be2[layer]), (L.aw[:, 0, :], aw[layer, 0:D]),
                                 (L.aw[:, 1, :], aw[layer, D:2 * D]), (L.ab[:, :], ab[layer:layer + 1])):
                    sp.dma_start(dst, src.partition_broadcast(P)).then_inc(L.s_w_in, 16)

            def load_x(b, par):
                rows = x_in[bass.ds(b * NCH, NCH)]
                sp.dma_start(L.x[:, par, :, :].rearrange("p (c t) d -> p c t d", c=NCH),
                             rows.rearrange("c p t d -> p c t d")).then_inc(L.s_x_in, 16)

            def load_mask(b, s):
                sp.dma_start(L.mask[s % TC][:, :], mask[b * NT + s % NT]).then_inc(L.s_mask[s % TC], 16)

            load_x(0, 0)
            for s in range(TC):
                load_mask(0, s)

            def emit(b, h, att, ffn, rt, old):
                u, c = NT * b + TC * h, NCH * b + h
                if att and h == 0:
                    if not (isinstance(b, int) and b == 0):
                        sp.wait_ge(L.s_ln, 4 * (u0 + u))
                    sp.wait_ge(L.s_x_in, 16 * (n_batch + b + 1))
                    load_x((b + 1) % B, (b + 1) % 2)
                if old and last:
                    if not (isinstance(c, int) and c == 3):
                        sp.wait_ge(L.s_fin, 4 * (c - 3))
                    sp.dma_start(L.x1[:, :, :], x1[c - 3]).then_inc(L.s_x1_in, 16)
                if att:
                    for q in range(TC):
                        s = TC * h + q
                        sp.wait_ge(L.s_masked, u_prep + u + q + 1)
                        load_mask(b if h == 0 else (b + 1) % B, s + TC)
                        if q == 1 and old:
                            store(c - 3)
                elif old:
                    store(c - 3)

            def store(k):
                if last:
                    sp.wait_ge(L.s_fin, 4 * (k + 1))
                else:
                    sp.wait_ge(L.s_xo, 2 * (c0 + k + 1))
                sp.dma_start(x_out[k], L.xo[:, :, :]).then_inc(L.s_xst, 16)

            batches(emit, sp.Fori)
            sp.wait_ge(L.s_xst, 16 * (c0 + C))
            sp.wait_ge(L.s_x_in, 16 * (n_batch + B + 1))
            for i in range(TC):
                sp.wait_ge(L.s_mask[i], 16 * (m0 + (U + TC) // TC))

        @block.gpsimd
        def _(pool):
            if layer == 0:
                make_identity(pool, L.ident, L.s_ident)
                pool.memset(L.half[:, :], -0.5).then_inc(L.s_half, 1)
                pool.memset(L.eps[:, :], EPS).then_inc(L.s_half, 1)
                for i in range(2):
                    pool.memset(L.x_hi[:, i, :, D:D + 1].bitcast(F32), 1.0).then_inc(L.s_ones, 1)
                    pool.memset(L.x_hi[:, i, :, D + 1:DE].bitcast(F32), 0.0).then_inc(L.s_ones, 1)
                pool.wait_ge(L.s_half, 2)

            def x_lo(n, par, v):
                pool.wait_ge(L.s_x_hi, NT * (n_batch + n) + v + 1)
                pool.tensor_tensor(L.x_lo[:, par, v, :], L.x[:, par, v, :], L.x_hi[:, par, v, 0:D].bitcast(F32),
                                   ALU.subtract).then_inc(L.s_x_lo, 1)

            for v in range(NT):
                x_lo(0, 0, v)

            def emit(b, h, att, ffn, rt, old):
                u, c = NT * b + TC * h, NCH * b + h
                for q in range(TC):
                    s = TC * h + q
                    if q == 0 and ffn:
                        for k in range(KD):
                            pool.wait_ge(L.s_h, 2 * (KD * (c0 + c - 1) + k + 1))
                            pool.tensor_tensor(L.h_lo[:, k, :], L.h[:, k, :], L.h_hi[:, k, :].bitcast(F32),
                                               ALU.subtract).then_inc(L.s_h_lo, 1)
                    if att:
                        pool.wait_ge(L.s_ln, 4 * (u0 + u + q + 1))
                        i = q % 2
                        pool.tensor_tensor(L.ve[:, i:i + 1], L.mv[:, i, 1:2], L.eps[:, 0:1], ALU.add).then_inc(L.s_rs, 1)
                        pool.wait_ge(L.s_rs, 2 * (u0 + u + q) + 1)
                        pool.tensor_tensor(L.rstd[:, i:i + 1], L.ve[:, i:i + 1], L.half[:, 0:1], ALU.pow).then_inc(L.s_rs, 1)
                    if q == 1 and ffn:
                        for f in range(KF):
                            pool.wait_ge(L.s_gelu, 2 * (KF * (c0 + c - 1) + f + 1))
                            pool.tensor_tensor(L.g_lo[:, f, :], L.g[:, f % G_RING, :], L.g_hi[:, f, :].bitcast(F32),
                                               ALU.subtract).then_inc(L.s_g_lo, 1)
                    if q == 1 and old and last:
                        pool.wait_ge(L.s_x1_in, 16 * (c - 2))
                        pool.wait_ge(L.s_xo, 2 * (c0 + c - 2))
                        pool.tensor_tensor(L.xo[:, :, :], L.xo[:, :, :], L.x1[:, :, :], ALU.add).then_inc(L.s_fin, 1)
                        pool.wait_ge(L.s_fin, 4 * (c - 3) + 3)
                        pool.tensor_tensor(L.ve2[:, :], L.mv2[:, :, 1], L.eps[:, :], ALU.add).then_inc(L.s_rs2, 1)
                        pool.wait_ge(L.s_rs2, rs2(c - 3, 1) + 1)
                        pool.tensor_tensor(L.rstd2[:, :], L.ve2[:, :], L.half[:, :], ALU.pow).then_inc(L.s_rs2, 1)
                    if q == 2 and rt:
                        k = c0 + c - 2
                        pool.wait_ge(L.s_ln2, 2 * TC * (k + 1))
                        pool.tensor_tensor(L.ve2[:, :], L.mv2[:, :, 1], L.eps[:, :], ALU.add).then_inc(L.s_rs2, 1)
                        pool.wait_ge(L.s_rs2, rs2(c - 2, 0) + 1)
                        pool.tensor_tensor(L.rstd2[:, :], L.ve2[:, :], L.half[:, :], ALU.pow).then_inc(L.s_rs2, 1)
                    if att:
                        for v in lo_beside.get(s, ()):
                            x_lo(b + 1, (b + 1) % 2, v)
                    if q == 3 and rt:
                        k = c0 + c - 2
                        pool.wait_ge(L.s_n2, k + 1)
                        pool.tensor_tensor(L.xo[:, :, :], L.xo[:, :, :],
                                           L.g2[:, :].unsqueeze(1).to_broadcast([P, TC, D]), ALU.mult).then_inc(L.s_xo, 1)
                        pool.wait_ge(L.s_xo, 2 * k + 1)
                        pool.tensor_tensor(L.xo[:, :, :], L.xo[:, :, :],
                                           L.be2[:, :].unsqueeze(1).to_broadcast([P, TC, D]), ALU.add).then_inc(L.s_xo, 1)

            batches(emit, pool.Fori)

        @block.scalar
        def _(act):
            act.wait_ge(L.s_w_in, 16 * 13 * (layer + 1))
            for k in range(KD):
                act.activation(L.w1[0][:, k, :], (L.t[k])[:, :], ACT.Copy).then_inc(L.s_w_hi, 1)
            for k in range(KD):
                fs = slice(k * KF // KD, (k + 1) * KF // KD)
                act.activation(L.w2[0][:, fs, :], L.t[KD + k][:, :].rearrange("p (f d) -> p f d", d=D), ACT.Copy)\
                   .then_inc(L.s_w_hi, 1)

            def pt_hi(u, i, first):
                if not first:
                    act.wait_ge(L.s_agg, u0 + u - 1)
                for g in range(2):
                    act.wait_ge(L.s_tr, 2 * (u_tr + u) + g + 1)
                    gs = slice(g * BANK, (g + 1) * BANK)
                    act.activation(L.pT[i][0][:, gs], L.PT[:, gs], ACT.Copy).then_inc(L.s_pt_hi, 1)

            def exp(u, s):
                i = s % TC
                act.wait_ge(L.s_nmx, u_prep + u + 1)
                act.activation(L.t[i][:, :], L.t[i][:, :], ACT.Exp, bias=L.nmx[:, i:i + 1]).then_inc(L.s_probs, 1)

            def sj_row(n):
                act.wait_ge(L.s_sjT, n_batch + n + 1)
                if not (isinstance(n, int) and n == 0):
                    act.wait_ge(L.s_score, u_prep + NT * n)
                act.activation(L.sj_row[:, 0, :], L.M[:, :], ACT.Copy).then_inc(L.s_sj_row, 1)

            sj_row(0)
            for s in range(AHEAD - 1):
                exp(s, s)
            pt_hi(0, 0, True)

            def emit(b, h, att, ffn, rt, old):
                u, c = NT * b + TC * h, NCH * b + h
                for q in range(TC):
                    s = TC * h + q
                    if att:
                        pt_hi(u + q + 1, (q + 1) % 2, isinstance(b, int) and b == 0 and s == 0)
                    if q == 0 and ffn:
                        k0 = KD * (c0 + c - 1)
                        if not (isinstance(c, int) and c == 1):
                            act.wait_ge(L.s_res, k0)
                        for k in range(KD):
                            act.wait_ge(L.s_hT, k0 + k + 1)
                            for dst in (L.h, L.h_hi):
                                act.activation(dst[:, k, :], L.M[:, k * BANK:(k + 1) * BANK], ACT.Identity,
                                               bias=L.be1[:, k:k + 1], scale=L.g1[:, k:k + 1]).then_inc(L.s_h, 1)
                    if att:
                        exp(u + q + 2, s + 2)
                        if s == TC:
                            sj_row(b + 1)
                    if q == 1 and ffn:
                        k0 = KF * (c0 + c - 1)
                        if not (isinstance(c, int) and c == 1):
                            act.wait_ge(L.s_ffn2, KD * (c0 + c - 1))
                        for f in range(KF):
                            act.wait_ge(L.s_ffn1, k0 + f + 1)
                            if f >= G_RING:
                                act.wait_ge(L.s_g_lo, k0 + f + 1 - G_RING)
                            for dst in (L.g[:, f % G_RING, :], L.g_hi[:, f, :]):
                                act.activation(dst, L.G[f % 2][:, :], ACT.Gelu, bias=L.b1[:, f:f + 1])\
                                   .then_inc(L.s_gelu, 1)

            batches(emit, act.Fori)

        @block.vector
        def _(dve):
            for k in range(KD):
                dve.wait_ge(L.s_w_hi, 2 * KD * layer + k + 1)
                dve.tensor_tensor(L.w1[1][:, k, :], L.t[k][:, :], L.w1[0][:, k, :].bitcast(F32), ALU.subtract)\
                   .then_inc(L.s_w_lo, 1)
            for k in range(KD):
                fs = slice(k * KF // KD, (k + 1) * KF // KD)
                dve.wait_ge(L.s_w_hi, 2 * KD * layer + KD + k + 1)
                dve.tensor_tensor(L.w2[1][:, fs, :], L.t[KD + k][:, :].rearrange("p (f d) -> p f d", d=D),
                                  L.w2[0][:, fs, :].bitcast(F32), ALU.subtract).then_inc(L.s_w_lo, 1)

            def prep_tile(n, par, v):
                if v == 0:
                    dve.wait_ge(L.s_x_in, 16 * (n_batch + n + 1))
                dve.tensor_copy(L.x_hi[:, par, v, 0:D], L.x[:, par, v, :]).then_inc(L.s_x_hi, 1)
                for half, dst in ((0, L.si), (1, L.sj)):
                    if 2 * v + half >= 2:
                        dve.wait_ge(L.s_sj, 2 * (NT * (n_batch + n) + v) + half - 1)
                    dve.scalar_tensor_tensor(L.prod[:, half, :], L.x[:, par, v, :], 1.0, L.aw[:, half, :], ALU.mult,
                                             ALU.mult, accum_out=dst[:, v:v + 1]).then_inc(L.s_sj, 1)

            def prep_batch(n, first):
                dve.wait_ge(L.s_sj, 2 * NT * (n_batch + n + 1))
                if not first:
                    dve.wait_ge(L.s_score, u_prep + NT * n)
                dve.tensor_scalar(L.a8[:, :], L.si[:, :], L.ab[:, :], 1.0 - SLOPE, ALU.add, ALU.mult).then_inc(L.s_prep, 1)
                dve.wait_ge(L.s_sj_row, n_batch + n + 1)
                dve.tensor_scalar(L.sj_row[:, 1, :], L.sj_row[:, 0, :], SLOPE, None, ALU.mult).then_inc(L.s_prep, 1)
                dve.wait_ge(L.s_prep, 2 * (n_batch + n + 1))

            def masked(u, s, k):
                i = s % TC
                t = L.t[i][:, :]
                if not (isinstance(u, int) and u < TC):
                    dve.wait_ge(L.s_tr, 2 * (u_tr + u + 1 - TC))
                dve.scalar_tensor_tensor(t, L.sj_row[:, 0, :], L.a8[:, s:s + 1], L.sj_row[:, 1, :], ALU.add,
                                         ALU.max).then_inc(L.s_score, 1)
                wait_alone(dve, L.s_passed, (L.s_score, u_prep + u + 1), (L.s_mask[i], 16 * (m0 + k + 1)))
                dve.tensor_tensor_reduce(out=t, in0=t, in1=L.mask[i][:, :], scale=1.0, scalar=LOWEST, op0=ALU.add,
                                         op1=ALU.max, accum_out=L.mx[:, i:i + 1]).then_inc(L.s_masked, 1)
                dve.wait_ge(L.s_masked, u_prep + u + 1)
                dve.tensor_scalar(L.nmx[:, i:i + 1], L.mx[:, i:i + 1], -1.0, None, ALU.mult).then_inc(L.s_nmx, 1)

            def pt_lo(u, i):
                for g in range(2):
                    dve.wait_ge(L.s_pt_hi, 2 * (u_tr + u) + g + 1)
                    gs = slice(g * BANK, (g + 1) * BANK)
                    dve.tensor_tensor(L.pT[i][1][:, gs], L.PT[:, gs], L.pT[i][0][:, gs].bitcast(F32), ALU.subtract)\
                       .then_inc(L.s_pt_lo, 1)

            def norm1_stats(u, s, par):
                i = s % 2
                n = 4 * (u0 + u)
                dve.wait_ge(L.s_agg, u0 + u + 1)
                dve.reciprocal(L.rinv[:, :], L.A[:, D:D + 1]).then_inc(L.s_ln, 1)
                dve.wait_ge(L.s_ln, n + 1)
                if not (isinstance(u, int) and u < 2):
                    dve.wait_ge(L.s_n1, u0 + u - 1)
                dve.scalar_tensor_tensor(L.u[:, i, :], L.A[:, 0:D], L.rinv[:, :], L.x[:, par, s, :], ALU.mult, ALU.add)\
                   .then_inc(L.s_ln, 1)
                dve.wait_ge(L.s_ln, n + 2)
                dve.bn_stats(L.st[:, i, :], L.u[:, i, :]).then_inc(L.s_ln, 1)
                wait_alone(dve, L.s_passed, (L.s_ln, n + 3))
                dve.bn_aggr(L.mv[:, i, :], L.st[:, i, :]).then_inc(L.s_ln, 1)

            def norm1_rows(u, h, q):
                i = q % 2
                dve.wait_ge(L.s_rs, 2 * (u0 + u + 1))
                dve.tensor_scalar(L.n1[:, h, q, :], L.u[:, i, :], L.mv[:, i, 0:1], L.rstd[:, i:i + 1], ALU.subtract,
                                  ALU.mult).then_inc(L.s_n1, 1)

            for v in range(NT):
                prep_tile(0, 0, v)
            prep_batch(0, True)
            dve.wait_ge(L.s_w_lo, 2 * KD * (layer + 1))
            for s in range(AHEAD):
                masked(s, s, 0)
            pt_lo(0, 0)

            def emit(b, h, att, ffn, rt, old):
                u, c = NT * b + TC * h, NCH * b + h
                for q in range(TC):
                    s = TC * h + q
                    if q == 2 and rt:
                        k = c0 + c - 2
                        dve.wait_ge(L.s_rt, k + 1)
                        for t in range(TC):
                            dve.bn_stats(L.st2[:, t, :], L.M[:, t * D:(t + 1) * D]).then_inc(L.s_ln2, 1)
                        wait_alone(dve, L.s_passed, (L.s_ln2, 2 * TC * k + TC))
                        for t in range(TC):
                            dve.bn_aggr(L.mv2[:, t, :], L.st2[:, t, :]).then_inc(L.s_ln2, 1)
                    if q == 3 and rt:
                        k = c0 + c - 2
                        dve.wait_ge(L.s_rs2, rs2(c - 2, 0) + 2)
                        if not (isinstance(c, int) and c == 2 and layer == 0):
                            dve.wait_ge(L.s_xst, 16 * k)
                        for t in range(TC):
                            mm = dve.tensor_scalar(L.xo[:, t, :], L.M[:, t * D:(t + 1) * D], L.mv2[:, t, 0:1],
                                                   L.rstd2[:, t:t + 1], ALU.subtract, ALU.mult)
                        mm.then_inc(L.s_n2, 1)
                    if att:
                        v = s + AHEAD
                        if v == NT:
                            prep_batch(b + 1, False)
                        if q < 3:
                            masked(u + q + AHEAD, v % NT, NCH * b + v // TC)
                        pt_lo(u + q + 1, (q + 1) % 2)
                        if q >= 1:
                            norm1_rows(u + q - 1, h, q - 1)
                        norm1_stats(u + q, s, b % 2)
                        if q == 3:
                            masked(u + q + AHEAD, v % NT, NCH * b + v // TC)
                            norm1_rows(u + q, h, q)
                        if s == 1:
                            for v in range(NT):
                                prep_tile(b + 1, (b + 1) % 2, v)
                    if q == 1 and old and last:
                        dve.wait_ge(L.s_fin, 4 * (c - 3) + 1)
                        for t in range(TC):
                            mm = dve.bn_stats(L.st2[:, t, :], L.xo[:, t, :])
                        mm.then_inc(L.s_fin, 1)
                        wait_alone(dve, L.s_passed, (L.s_fin, 4 * (c - 3) + 2))
                        for t in range(TC):
                            mm = dve.bn_aggr(L.mv2[:, t, :], L.st2[:, t, :])
                        mm.then_inc(L.s_fin, 1)
                        dve.wait_ge(L.s_rs2, rs2(c - 3, 1) + 2)
                        for t in range(TC):
                            mm = dve.tensor_scalar(L.xo[:, t, :], L.xo[:, t, :], L.mv2[:, t, 0:1], L.rstd2[:, t:t + 1],
                                                   ALU.subtract, ALU.mult)
                        mm.then_inc(L.s_fin, 1)
                    if q >= 2 and ffn:
                        k = q - 2
                        n = KD * (c0 + c - 1) + k
                        dve.wait_ge(L.s_ffn2, n + 1)
                        if not (isinstance(c, int) and c == 1):
                            dve.wait_ge(L.s_rt, c0 + c - 1)
                        dve.scalar_tensor_tensor(L.rT[:, k, :], L.Y[:, :], L.b2[:, k:k + 1], L.h[:, k, :], ALU.add,
                                                 ALU.add).then_inc(L.s_res, 1)
            batches(emit, dve.Fori)

        @block.tensor
        def _(pe):
            pe.wait_ge(L.s_ident, 2)
            pe.wait_ge(L.s_ones, 4)

            def transpose_probs(u, s, first):
                pe.wait_ge(L.s_probs, u_exp + u + 1)
                for g in range(2):
                    if not first:
                        pe.wait_ge(L.s_pt_lo, 2 * (u_tr + u) - 1 + g)
                    for q in range(TC):
                        js = slice((TC * g + q) * P, (TC * g + q + 1) * P)
                        mm = pe.transpose(L.PT[:, js], L.t[s % TC][:, js], L.ident[:, :])
                    mm.then_inc(L.s_tr, 1)

            def aggregate(u, i, b, par, first):
                pe.wait_ge(L.s_pt_lo, 2 * (u_tr + u + 1))
                if not first:
                    pe.wait_ge(L.s_ln, 4 * (u0 + u) - 2)
                for j in range(NT):
                    js = slice(j * P, (j + 1) * P)
                    hi, lo = L.pT[i][0][:, js], L.pT[i][1][:, js]
                    pe.matmul(L.A[:, 0:DE], hi, L.x_hi[:, par, j, :], start=(j == 0), stop=False)
                    pe.matmul(L.A[:, 0:DE], lo, L.x_hi[:, par, j, :], start=False, stop=False)
                    mm = pe.matmul(L.A[:, 0:D], hi, L.x_lo[:, par, j, :], start=False, stop=(j == NT - 1))
                mm.then_inc(L.s_agg, 1)

            def sj_row(n):
                pe.wait_ge(L.s_sj, 2 * NT * (n_batch + n + 1))
                for v in range(NT):
                    mm = pe.transpose(L.M[:, v * P:(v + 1) * P], L.sj[:, v:v + 1].to_broadcast([P, P]), L.ident[:, :])
                mm.then_inc(L.s_sjT, 1)

            sj_row(0)
            pe.wait_ge(L.s_w_lo, 2 * KD * (layer + 1))
            transpose_probs(0, 0, True)

            def emit(b, h, att, ffn, rt, old):
                u, c = NT * b + TC * h, NCH * b + h
                start = isinstance(c, int) and c == 0
                for q in range(TC):
                    s = TC * h + q
                    if att:
                        transpose_probs(u + q + 1, q + 1, False)
                    if q == 0 and ffn:
                        k0 = c0 + c - 1
                        pe.wait_ge(L.s_n1, TC * (k0 + 1))
                        if isinstance(c, int) and c <= 2:
                            pe.wait_ge(L.s_sj_row, n_batch + c)
                        else:
                            pe.wait_ge(L.s_n2, k0 - 1)
                        for k in range(KD):
                            for t in range(TC):
                                mm = pe.transpose(L.M[:, k * BANK + t * P:k * BANK + (t + 1) * P],
                                                  L.n1[:, (h + 1) % 2, t, k * P:(k + 1) * P], L.ident[:, :])
                            mm.then_inc(L.s_hT, 1)
                    if att:
                        if s == 0:
                            pe.wait_ge(L.s_x_lo, NT * (n_batch + b + 1))
                        aggregate(u + q, q % 2, b, b % 2, start and q == 0)
                        if s == TC:
                            pe.wait_ge(L.s_h, 2 * KD * (c0 + c))
                            sj_row(b + 1)
                    if q == 1 and ffn:
                        k0 = c0 + c - 1
                        pe.wait_ge(L.s_h_lo, KD * (k0 + 1))
                        for f in range(KF):
                            n = KF * k0 + f
                            if not (isinstance(c, int) and c == 1 and f < 2 and layer == 0):
                                pe.wait_ge(L.s_gelu, 2 * (n - 1))
                            fs = slice(f * P, (f + 1) * P)
                            for k in range(KD):
                                mm = split_product(pe, L.G[f % 2][:, :], (L.w1[0][:, k, fs], L.w1[1][:, k, fs]),
                                                   (L.h_hi[:, k, :], L.h_lo[:, k, :]), k == 0, k == KD - 1)
                            mm.then_inc(L.s_ffn1, 1)
                    if q == 1 and rt:
                        k0 = c0 + c - 2
                        if att and h == 1:
                            pe.wait_ge(L.s_sj_row, n_batch + b + 2)
                        elif ffn:
                            pe.wait_ge(L.s_h, 2 * KD * (k0 + 2))
                        else:
                            pe.wait_ge(L.s_n2, k0)
                        pe.wait_ge(L.s_res, KD * (k0 + 1))
                        for t in range(TC):
                            for k in range(KD):
                                mm = pe.transpose(L.M[:, t * D + k * P:t * D + (k + 1) * P],
                                                  L.rT[:, k, t * P:(t + 1) * P], L.ident[:, :])
                        mm.then_inc(L.s_rt, 1)
                    if q >= 2 and ffn:
                        k0 = c0 + c - 1
                        o = q - 2
                        pe.wait_ge(L.s_g_lo, KF * (k0 + 1))
                        if not (isinstance(c, int) and c == 1 and o == 0):
                            pe.wait_ge(L.s_res, KD * k0 + o)
                        os = slice(o * P, (o + 1) * P)
                        for f in range(KF):
                            mm = split_product(pe, L.Y[:, :], (L.w2[0][:, f, os], L.w2[1][:, f, os]),
                                               (L.g_hi[:, f, :], L.g_lo[:, f, :]), f == 0, f == KF - 1)
                        mm.then_inc(L.s_ffn2, 1)

            batches(emit, pe.Fori)


def program(nc, x, adj, L0_W, L0_b, L0_attn, attn_w, attn_b, W1, b1, W2, b2, g1, beta1, g2, beta2, out):
    B, N, D, _, NT, _, _ = shapes(x, W1)
    TC = BANK // P
    C = B * N // BANK
    rows = [nc.dram_tensor(f"rows{i}", (C * TC, P, D), F32, kind="Internal").ap() for i in range(3)]
    mask = nc.dram_tensor("mask", (B * NT, P, N), BF16, kind="Internal").ap()
    chunks = [r.rearrange("(c t) p d -> c p t d", t=TC) for r in rows]
    chunks.append(out.rearrange("b (c t p) d -> (b c) p t d", t=TC, p=P))
    first_stage(nc, x, adj, L0_W, L0_b, L0_attn, rows[0], mask, W1)
    par = (attn_w, attn_b, W1, b1, W2, b2, g1, beta1, g2, beta2)
    layers = W1.shape[0]
    with ExitStack() as ctx:
        L = layer_buffers(nc, ctx, x, W1)
        for layer in range(layers):
            graph_layer(nc, L, layer, x, chunks[layer], chunks[layer + 1], chunks[0], mask, par, layer == layers - 1)


_INS = ['x', 'adj', 'L0_gnn_W', 'L0_gnn_b', 'L0_gnn_attn', 'L1_gnn_attn_w', 'L1_gnn_attn_b', 'L1_gnn_W1', 'L1_gnn_b1',
        'L1_gnn_W2', 'L1_gnn_b2', 'L1_gnn_g1', 'L1_gnn_beta1', 'L1_gnn_g2', 'L1_gnn_beta2']


def kernel(**inputs):
    import numpy as _np
    import concourse.bacc as _bacc
    from concourse import mybir as _mybir
    from concourse.bass_utils import run_bass_kernel_spmd as _run

    nc = _bacc.Bacc("TRN2", target_bir_lowering=False, num_devices=1)
    arrays, args = {}, []
    for name in _INS:
        a = _np.ascontiguousarray(inputs[name])
        arrays[f"in_{name}"] = a
        args.append(nc.dram_tensor(f"in_{name}", a.shape, _mybir.dt.from_np(a.dtype), kind="ExternalInput").ap())
    shape = inputs["x"].shape
    args.append(nc.dram_tensor("out_rows", shape, _mybir.dt.float32, kind="ExternalOutput").ap())
    program(nc, *args)
    r = _run(nc, [arrays], core_ids=[0])
    return r.results[0]["out_rows"]
```

```python
from contextlib import ExitStack

import concourse.bass as bass
from concourse import mybir


P = 128
F32 = mybir.dt.float32
F32R = mybir.dt.float32r
BF16 = mybir.dt.bfloat16
I32 = mybir.dt.int32
ALU = mybir.AluOpType
ACT = mybir.ActivationFunctionType

MASKED = -1.0e30
LOWEST = -3.0e38
EPS = 1e-5
SLOPE = 0.2
BANK = 512
AHEAD = 3
G_RING = 3


def shapes(x, w1):
    B, N, D = x.shape
    F = w1.shape[2]
    return B, N, D, F, N // P, D // P, F // P


def split_product(pe, out, hi_lo_left, hi_lo_right, start, stop):
    (left_hi, left_lo), (right_hi, right_lo) = hi_lo_left, hi_lo_right
    pe.matmul(out, left_hi, right_hi, start=start, stop=False)
    pe.matmul(out, left_lo, right_hi, start=False, stop=False)
    return pe.matmul(out, left_hi, right_lo, start=False, stop=stop)


def wait_alone(eng, passed, *waits):
    for sem, value in waits:
        eng.wait_ge(sem, value)
    eng.sem_inc(passed, 1)


def make_identity(pool, ident, done):
    pool.memset(ident[:, :], 0.0).then_inc(done, 1)
    pool.wait_ge(done, 1)
    pool.affine_select(out=ident[:, :], in_=ident[:, :], compare_op=ALU.not_equal, fill=1.0,
                       base=0, pattern=[[-1, P]], channel_multiplier=1).then_inc(done, 1)


def first_stage(nc, x, adj, W, bias, attn, x1_dram, mask_dram, w1, xr, s_next_x):
    B, N, D, _, NT, KD, _ = shapes(x, w1)
    NC = N // BANK
    TC = BANK // P
    DE = D + 2
    AR = 2
    PJ = 4 * NC * KD
    SCORED = 3 * NC * KD
    assert PJ == 2 * NT and B % 2 == 0 and NT % 2 == 0
    with ExitStack() as ctx:
        def sb(name, shape, dt=F32):
            return ctx.enter_context(nc.sbuf_tensor("a_" + name, shape, dt))

        def sem(name):
            return ctx.enter_context(nc.semaphore("a_" + name))

        ident = sb("ident", [P, P])
        ident_r = sb("ident_r", [P, P], F32R)
        ident_i = sb("ident_i", [P, P], I32)
        w_in = sb("w_in", [P, KD, D])
        at_in = sb("at_in", [P, KD, D])
        bias_col = sb("bias_col", [P, KD])
        wT = [sb("wT_hi", [P, KD, D], F32R), sb("wT_lo", [P, KD, D], F32R)]
        at = [sb("at_hi", [P, KD, D], F32R), sb("at_lo", [P, KD, D], F32R)]
        xs = sb("xs", [P, NT, D])
        xT = [sb("xT_hi", [P, KD, N], F32R), sb("xT_lo", [P, KD, N], F32R)]
        hT = [[sb(f"hT_hi{i}", [P, KD, N], F32R), sb(f"hT_lo{i}", [P, KD, N], F32R)] for i in range(2)]
        haT = [[sb(f"haT_hi{i}", [P, KD, N], F32R), sb(f"haT_lo{i}", [P, KD, N], F32R)] for i in range(2)]
        hn = [[sb(f"hn_hi{i}", [P, NT, DE], F32R), sb(f"hn_lo{i}", [P, NT, D], F32R)] for i in range(2)]
        adj_t = sb("adj_t", [P, AR, N], I32)
        mask0 = sb("mask0", [P, 2, N], BF16)
        mask1 = sb("mask1", [P, 2, N], BF16)
        t = [sb(f"t{i}", [P, N]) for i in range(2)]
        pT = [[sb(f"pT_hi{i}", [P, N], F32R), sb(f"pT_lo{i}", [P, N], F32R)] for i in range(2)]
        mx = sb("mx", [P, 2])
        nmx = sb("nmx", [P, 2])
        rinv = sb("rinv", [P, 2])
        z = sb("z", [P, 2, D])
        neg = sb("neg", [P, 2, D])
        y = sb("y", [P, 2, D])
        stats = sb("stats", [P, 2, 6])
        mv = sb("mv", [P, 2, 2])
        ve = sb("ve", [P, 2])
        rstd = sb("rstd", [P, 2])
        half = sb("half", [P, 1])
        eps = sb("eps", [P, 1])
        xo = sb("xo", [P, 2, D])

        S = [ctx.enter_context(nc.psum_tensor(f"a_S{i}", [P, N], F32)) for i in range(2)]
        PT = ctx.enter_context(nc.psum_tensor("a_PT", [P, N], F32))
        O = ctx.enter_context(nc.psum_tensor("a_O", [P, BANK], F32))
        J = ctx.enter_context(nc.psum_tensor("a_J", [P, BANK], F32))

        s_id = sem("ident")
        s_idr = sem("ident_copies")
        s_half = sem("half")
        s_ones = sem("ones")
        s_w = sem("weights_in")
        s_wt = sem("w_transposed")
        s_whi = sem("weights_hi")
        s_wlo = sem("weights_lo")
        s_xs = sem("xs_in")
        s_xr = sem("xr_in")
        s_adj = [sem(f"adj_in{i}") for i in range(AR)]
        s_mask0 = sem("mask0")
        s_mask = sem("mask_step")
        s_mst = [sem(f"mask_stored{i}") for i in range(2)]
        s_mm = sem("proj_product")
        s_phi = sem("proj_hi")
        s_plo = sem("proj_lo")
        s_s = sem("scores")
        s_t = sem("masked")
        s_nm = sem("max_negated")
        s_p = sem("probs")
        s_tr = sem("probs_transposed")
        s_thi = sem("probsT_hi")
        s_tlo = sem("probsT_lo")
        s_pv = sem("values")
        s_rinv = sem("rinv")
        s_z = sem("values_scaled")
        s_neg = sem("negative_part")
        s_ln = sem("norm_step")
        s_ex = sem("elu_exp")
        s_passed = sem("passed")
        s_passed_pool = sem("passed_pool")
        s_rs = sem("rstd_step")
        s_st = [sem(f"x1_stored{i}") for i in range(2)]
        LN = 5

        def batches(emit, loop):
            emit(0, 0, True, False)
            with loop(0, (B - 2) // 2) as i:
                for j in (1, 2):
                    emit(2 * i + j, j % 2, False, False)
            emit(B - 1, 1, False, True)

        def bank(b, p):
            return O if isinstance(b, int) and b == 0 and p % 2 == 1 else J

        block = ctx.enter_context(nc.Block())

        @block.sync
        def _(sp):
            def load_adj(b, k):
                sp.dma_start(adj_t[:, k % AR, :], adj[b, k * P:(k + 1) * P, :]).then_inc(s_adj[k % AR], 16)

            def load_xs(b):
                sp.dma_start(xs[:, :, :], x[b].rearrange("(t p) d -> p t d", p=P)).then_inc(s_xs, 16)

            def load_xr(b, par):
                sp.dma_start(xr[:, par, :, :], x[b].rearrange("(t p) d -> p t d", p=P)).then_inc(s_xr, 16)

            def store_mask(b, k):
                sp.dma_start(mask_dram[b * NT + k], mask1[:, k % 2, :]).then_inc(s_mst[k % 2], 16)

            def store_x1(b, k):
                sp.wait_ge(s_ln, LN * (NT * b + k + 1))
                sp.dma_start(x1_dram[b * NT + k], xo[:, k % 2, :]).then_inc(s_st[k % 2], 16)

            sp.dma_start(w_in[:, :, :], W.rearrange("(k p) i -> p k i", p=P)).then_inc(s_w, 16)
            sp.dma_start(at_in[:, :, :], attn.rearrange("(k p) j -> p k j", p=P)).then_inc(s_w, 16)
            with nc.allow_non_contiguous_dma("a column of the bias"):
                sp.dma_start(bias_col[:, :], bias.rearrange("(k p) -> p k", p=P)).then_inc(s_w, 16)
            load_xs(0)
            load_adj(0, 0)
            load_adj(0, 1)
            load_xr(0, 0)
            for k in range(2):
                sp.wait_ge(s_mask, 2 * (k + 1))
                load_adj(0, k + AR)
                store_mask(0, k)
            sp.wait_ge(s_mm, NC * KD)
            load_xs(1)

            def emit(b, par, first, last):
                for k in range(NT):
                    if not (last and k + 2 >= NT):
                        b2, k2 = b + (k + 2) // NT, (k + 2) % NT
                        sp.wait_ge(s_mask, 2 * (NT * b + k + 3))
                        if not (last and k + 4 >= NT):
                            load_adj(b + (k + 4) // NT, (k + 4) % NT)
                        store_mask(b2, k2)
                    if k == 2 and not last:
                        if not first:
                            sp.wait_ge(s_ln, LN * (NT * b - 1) + 1)
                        load_xr(b + 1, 1 - par)
                        sp.wait_ge(s_mm, PJ * (b + 1) + NC * KD)
                        load_xs((b + 2) % B)
                    if k == 2 and last:
                        sp.wait_ge(s_ln, LN * (NT * b - 1) + 1)
                        for i in range(2):
                            sp.wait_ge(s_st[i], 16 * NT // 2)
                        sp.dma_start(xr[:, 0, :, :], x1_dram[0:NT].rearrange("t p d -> p t d")).then_inc(s_next_x, 16)
                    if not first or k >= 2:
                        store_x1(b + (k - 2) // NT, (k - 2) % NT)

            batches(emit, sp.Fori)
            for k in (NT - 2, NT - 1):
                store_x1(B - 1, k)
            for i in range(2):
                sp.wait_ge(s_mst[i], 16 * B * NT // 2)
                sp.wait_ge(s_st[i], 16 * B * NT // 2)
            sp.wait_ge(s_xs, 16 * (B + 1))
            sp.wait_ge(s_next_x, 16)

        @block.gpsimd
        def _(pool):
            make_identity(pool, ident, s_id)
            pool.memset(half[:, :], -0.5).then_inc(s_half, 1)
            pool.memset(eps[:, :], EPS).then_inc(s_half, 1)
            for i in range(2):
                pool.memset(hn[i][0][:, :, D:D + 1].bitcast(F32), 1.0).then_inc(s_ones, 1)
                pool.memset(hn[i][0][:, :, D + 1:DE].bitcast(F32), 0.0).then_inc(s_ones, 1)
            pool.wait_ge(s_half, 2)
            pool.wait_ge(s_idr, 2)

            def mask1_tile(b, k, start):
                n = NT * b + k
                i, a = k % 2, k % AR
                pool.wait_ge(s_mask0, n + 1)
                dg = adj_t[:, a, k * P:(k + 1) * P]
                pool.tensor_tensor(dg, dg, ident_i[:, :], ALU.add).then_inc(s_mask, 1)
                if start:
                    wait_alone(pool, s_passed_pool, (s_mask, 2 * n + 1))
                else:
                    wait_alone(pool, s_passed_pool, (s_mask, 2 * n + 1), (s_mst[i], 16 * (NT // 2 * b + k // 2)))
                pool.tensor_scalar(mask1[:, i, :], adj_t[:, a, :], 0.0, MASKED, ALU.is_le, ALU.mult).then_inc(s_mask, 1)

            def deviation(b, k):
                n = NT * b + k
                i = k % 2
                pool.wait_ge(s_ln, LN * n + 4)
                pool.tensor_tensor(ve[:, i:i + 1], mv[:, i, 1:2], eps[:, :], ALU.add).then_inc(s_rs, 1)
                pool.wait_ge(s_rs, 2 * n + 1)
                pool.tensor_tensor(rstd[:, i:i + 1], ve[:, i:i + 1], half[:, :], ALU.pow).then_inc(s_rs, 1)

            for k in range(3):
                mask1_tile(0, k, k < 2)

            def emit(b, par, first, last):
                for k in range(NT):
                    if not (last and k + 3 >= NT):
                        mask1_tile(b + (k + 3) // NT, (k + 3) % NT, False)
                    if not (first and k == 0):
                        deviation(b + (k - 1) // NT, (k - 1) % NT)

            batches(emit, pool.Fori)
            deviation(B - 1, NT - 1)

        @block.scalar
        def _(act):
            act.wait_ge(s_w, 48)
            act.activation(at[0][:, :, :], at_in[:, :, :], ACT.Copy).then_inc(s_whi, 1)
            act.wait_ge(s_wt, KD * KD)
            for k in range(KD):
                act.activation(wT[0][:, k, :], PT[:, k * BANK:k * BANK + D], ACT.Copy).then_inc(s_whi, 1)

            def proj_hi(b, par, p):
                part, c, k = p // (NC * KD), p % (NC * KD) // KD, p % KD
                act.wait_ge(s_mm, PJ * b + p + 1)
                src = bank(b, p)[:, :]
                cs = slice(c * BANK, (c + 1) * BANK)
                if part == 0:
                    act.activation(xT[0][:, k, cs], src, ACT.Copy).then_inc(s_phi, 1)
                elif part == 1:
                    act.activation(hT[par][0][:, k, cs], src, ACT.Identity, bias=bias_col[:, k:k + 1]).then_inc(s_phi, 1)
                elif part == 2:
                    act.activation(haT[par][0][:, k, cs], src, ACT.Copy).then_inc(s_phi, 1)
                else:
                    g = p % (NC * KD)
                    act.activation(hn[par][0][:, 2 * g:2 * g + 2, 0:D], src.rearrange("p (t d) -> p t d", d=D),
                                   ACT.Copy).then_inc(s_phi, 1)

            def softmax_exp(b, k):
                act.wait_ge(s_nm, NT * b + k + 1)
                act.activation(t[k % 2][:, :], t[k % 2][:, :], ACT.Exp, bias=nmx[:, k % 2:k % 2 + 1]).then_inc(s_p, 1)

            def transposed_hi(b, k, start):
                if not start:
                    act.wait_ge(s_pv, NT * b + k - 1)
                for g in range(2):
                    act.wait_ge(s_tr, 2 * (NT * b + k) + g + 1)
                    gs = slice(g * BANK, (g + 1) * BANK)
                    act.activation(pT[k % 2][0][:, gs], PT[:, gs], ACT.Copy).then_inc(s_thi, 1)

            def scaled(b, k, start):
                n = NT * b + k
                i = k % 2
                act.wait_ge(s_rinv, n + 1)
                if not start:
                    act.wait_ge(s_ln, LN * (n - 2) + 1)
                act.activation(z[:, i, :], O[:, 0:D], ACT.Copy, scale=rinv[:, i:i + 1]).then_inc(s_z, 1)

            def elu_exp(b, k):
                act.wait_ge(s_neg, NT * b + k + 1)
                act.activation(neg[:, k % 2, :], neg[:, k % 2, :], ACT.Exp).then_inc(s_ex, 1)

            for p in range(PJ):
                proj_hi(0, 0, p)
            softmax_exp(0, 0)
            softmax_exp(0, 1)
            transposed_hi(0, 0, True)

            def emit(b, par, first, last):
                for k in range(NT):
                    before = (b + (k - 1) // NT, (k - 1) % NT)
                    if not (first and k == 0):
                        scaled(*before, first and k <= 2)
                    if not last:
                        proj_hi(b + 1, 1 - par, 2 * k)
                    if not (first and k == 0):
                        elu_exp(*before)
                    if not last:
                        proj_hi(b + 1, 1 - par, 2 * k + 1)
                    if not (last and k + 2 >= NT):
                        softmax_exp(b + (k + 2) // NT, (k + 2) % NT)
                    if not (last and k + 1 >= NT):
                        transposed_hi(b + (k + 1) // NT, (k + 1) % NT, first and k == 0)

            batches(emit, act.Fori)
            scaled(B - 1, NT - 1, False)
            elu_exp(B - 1, NT - 1)

        @block.vector
        def _(dve):
            dve.wait_ge(s_id, 2)
            dve.tensor_copy(ident_r[:, :], ident[:, :]).then_inc(s_idr, 1)
            dve.tensor_copy(ident_i[:, :], ident[:, :]).then_inc(s_idr, 1)
            dve.wait_ge(s_whi, 1)
            dve.tensor_tensor(at[1][:, :, :], at_in[:, :, :], at[0][:, :, :].bitcast(F32), ALU.subtract).then_inc(s_wlo, 1)
            for k in range(KD):
                dve.wait_ge(s_whi, 2 + k)
                dve.tensor_tensor(wT[1][:, k, :], PT[:, k * BANK:k * BANK + D], wT[0][:, k, :].bitcast(F32),
                                  ALU.subtract).then_inc(s_wlo, 1)

            def proj_lo(b, par, p):
                part, c, k = p // (NC * KD), p % (NC * KD) // KD, p % KD
                dve.wait_ge(s_phi, PJ * b + p + 1)
                src = bank(b, p)[:, :]
                cs = slice(c * BANK, (c + 1) * BANK)
                if part == 0:
                    dve.tensor_tensor(xT[1][:, k, cs], src, xT[0][:, k, cs].bitcast(F32), ALU.subtract).then_inc(s_plo, 1)
                elif part == 1:
                    dve.scalar_tensor_tensor(hT[par][1][:, k, cs], src, bias_col[:, k:k + 1],
                                             hT[par][0][:, k, cs].bitcast(F32), ALU.add, ALU.subtract).then_inc(s_plo, 1)
                elif part == 2:
                    dve.tensor_tensor(haT[par][1][:, k, cs], src, haT[par][0][:, k, cs].bitcast(F32),
                                      ALU.subtract).then_inc(s_plo, 1)
                else:
                    g = p % (NC * KD)
                    dve.tensor_tensor(hn[par][1][:, 2 * g:2 * g + 2, :], src.rearrange("p (t d) -> p t d", d=D),
                                      hn[par][0][:, 2 * g:2 * g + 2, 0:D].bitcast(F32), ALU.subtract).then_inc(s_plo, 1)

            def mask0_tile(b, k, start):
                dve.wait_ge(s_adj[k % AR], 16 * (NT // AR * b + k // AR + 1))
                if not start:
                    dve.wait_ge(s_t, NT * b + k - 1)
                dve.tensor_scalar(mask0[:, k % 2, :], adj_t[:, k % AR, :], 0.0, MASKED, ALU.is_equal, ALU.mult)\
                   .then_inc(s_mask0, 1)

            def masked_scores(b, k, start):
                n = NT * b + k
                i = k % 2
                dve.wait_ge(s_mask0, n + 1)
                if start:
                    wait_alone(dve, s_passed, (s_s, n + 1))
                else:
                    wait_alone(dve, s_passed, (s_s, n + 1), (s_tr, 2 * (n - 1)))
                dve.tensor_tensor_reduce(out=t[i][:, :], in0=S[i][:, :], in1=mask0[:, i, :], scale=1.0, scalar=LOWEST,
                                         op0=ALU.add, op1=ALU.max, accum_out=mx[:, i:i + 1]).then_inc(s_t, 1)
                dve.wait_ge(s_t, n + 1)
                dve.tensor_scalar(nmx[:, i:i + 1], mx[:, i:i + 1], -1.0, None, ALU.mult).then_inc(s_nm, 1)

            def transposed_lo(b, k):
                for g in range(2):
                    dve.wait_ge(s_thi, 2 * (NT * b + k) + g + 1)
                    gs = slice(g * BANK, (g + 1) * BANK)
                    dve.tensor_tensor(pT[k % 2][1][:, gs], PT[:, gs], pT[k % 2][0][:, gs].bitcast(F32),
                                      ALU.subtract).then_inc(s_tlo, 1)

            def inverse_sum(b, k):
                n = NT * b + k
                dve.wait_ge(s_pv, n + 1)
                dve.reciprocal(rinv[:, k % 2:k % 2 + 1], O[:, D:D + 1]).then_inc(s_rinv, 1)

            def negative_part(b, k, start):
                n = NT * b + k
                dve.wait_ge(s_z, n + 1)
                if not start:
                    dve.wait_ge(s_ln, LN * (n - 1) + 2)
                dve.tensor_scalar(neg[:, k % 2, :], z[:, k % 2, :], 0.0, None, ALU.min).then_inc(s_neg, 1)

            def residual_stats(b, par, k, start):
                n = NT * b + k
                i = k % 2
                if k == 0:
                    dve.wait_ge(s_xr, 16 * (b + 1))
                if not start:
                    dve.wait_ge(s_ln, LN * n)
                dve.wait_ge(s_z, n + 1)
                dve.scalar_tensor_tensor(y[:, i, :], z[:, i, :], 0.0, xr[:, par, k, :], ALU.max, ALU.add).then_inc(s_ln, 1)
                dve.wait_ge(s_ln, LN * n + 1)
                dve.wait_ge(s_ex, n + 1)
                dve.scalar_tensor_tensor(y[:, i, :], neg[:, i, :], -1.0, y[:, i, :], ALU.add, ALU.add).then_inc(s_ln, 1)
                dve.wait_ge(s_ln, LN * n + 2)
                dve.bn_stats(stats[:, i, :], y[:, i, :]).then_inc(s_ln, 1)
                wait_alone(dve, s_passed, (s_ln, LN * n + 3))
                dve.bn_aggr(mv[:, i, :], stats[:, i, :]).then_inc(s_ln, 1)

            def norm(b, k, start):
                n = NT * b + k
                i = k % 2
                dve.wait_ge(s_rs, 2 * n + 2)
                if not start:
                    dve.wait_ge(s_st[i], 16 * (NT // 2 * b + k // 2))
                dve.tensor_scalar(xo[:, i, :], y[:, i, :], mv[:, i, 0:1], rstd[:, i:i + 1], ALU.subtract,
                                  ALU.mult).then_inc(s_ln, 1)

            mask0_tile(0, 0, True)
            mask0_tile(0, 1, True)
            for p in range(PJ):
                proj_lo(0, 0, p)
            masked_scores(0, 0, True)
            masked_scores(0, 1, True)
            mask0_tile(0, 2, False)
            transposed_lo(0, 0)

            def emit(b, par, first, last):
                for k in range(NT):
                    before = (b + (k - 1) // NT, (k - 1) % NT)
                    if not (first and k == 0):
                        inverse_sum(*before)
                    if not (first and k <= 1):
                        norm(b + (k - 2) // NT, (k - 2) % NT, first and k <= 3)
                    if not last:
                        proj_lo(b + 1, 1 - par, 2 * k)
                    if not (first and k == 0):
                        negative_part(*before, first and k == 1)
                    if not (last and k + 3 >= NT):
                        mask0_tile(b + (k + 3) // NT, (k + 3) % NT, False)
                    if not (last and k + 2 >= NT):
                        masked_scores(b + (k + 2) // NT, (k + 2) % NT, False)
                    if not last:
                        proj_lo(b + 1, 1 - par, 2 * k + 1)
                    if not (first and k == 0):
                        residual_stats(before[0], par if k else 1 - par, before[1], first and k == 1)
                    if not (last and k + 1 >= NT):
                        transposed_lo(b + (k + 1) // NT, (k + 1) % NT)

            batches(emit, dve.Fori)
            inverse_sum(B - 1, NT - 1)
            norm(B - 1, NT - 2, False)
            negative_part(B - 1, NT - 1, False)
            residual_stats(B - 1, 1, NT - 1, False)
            norm(B - 1, NT - 1, False)

        @block.tensor
        def _(pe):
            pe.wait_ge(s_id, 2)
            pe.wait_ge(s_w, 48)
            for k in range(KD):
                for o in range(KD):
                    pe.transpose(PT[:, k * BANK + o * P:k * BANK + (o + 1) * P], w_in[:, o, k * P:(k + 1) * P],
                                 ident[:, :]).then_inc(s_wt, 1)
            pe.wait_ge(s_idr, 2)
            pe.wait_ge(s_wlo, 1 + KD)
            pe.wait_ge(s_ones, 4)

            def project(b, par, p, start):
                part, c, k = p // (NC * KD), p % (NC * KD) // KD, p % KD
                out = bank(b, p)
                if p == 0:
                    pe.wait_ge(s_xs, 16 * (b + 1))
                if not start:
                    pe.wait_ge(s_plo, PJ * b + p)
                elif p >= 2:
                    pe.wait_ge(s_plo, p - 1)
                if part == 0:
                    for q in range(TC):
                        mm = pe.transpose(out[:, q * P:(q + 1) * P], xs[:, TC * c + q, k * P:(k + 1) * P], ident[:, :])
                elif part in (1, 2):
                    src, w = (xT, wT) if part == 1 else (hT[par], at)
                    pe.wait_ge(s_plo, PJ * b + NC * KD * (part - 1) + KD * (c + 1))
                    cs, os = slice(c * BANK, (c + 1) * BANK), slice(k * P, (k + 1) * P)
                    for i in range(KD):
                        mm = split_product(pe, out[:, :], (w[0][:, i, os], w[1][:, i, os]),
                                           (src[0][:, i, cs], src[1][:, i, cs]), i == 0, i == KD - 1)
                else:
                    g = p % (NC * KD)
                    for q in range(2):
                        ts = slice((2 * g + q) * P, (2 * g + q + 1) * P)
                        for i in range(KD):
                            o = out[:, q * D + i * P:q * D + (i + 1) * P]
                            pe.matmul(o, hT[par][0][:, i, ts], ident_r[:, :], start=True, stop=False)
                            mm = pe.matmul(o, hT[par][1][:, i, ts], ident_r[:, :], start=False, stop=True)
                mm.then_inc(s_mm, 1)

            def scores(b, par, j, start):
                n = NT * b + j
                if j == 0:
                    pe.wait_ge(s_plo, PJ * b + SCORED)
                if not start:
                    pe.wait_ge(s_t, n - 1)
                ts = slice(j * P, (j + 1) * P)
                for c in range(NC):
                    cs = slice(c * BANK, (c + 1) * BANK)
                    for k in range(KD):
                        mm = split_product(pe, S[j % 2][:, cs], (haT[par][0][:, k, ts], haT[par][1][:, k, ts]),
                                           (hT[par][0][:, k, cs], hT[par][1][:, k, cs]), k == 0, k == KD - 1)
                mm.then_inc(s_s, 1)

            def transpose_probs(b, j, start):
                n = NT * b + j
                pe.wait_ge(s_p, n + 1)
                for g in range(2):
                    if not start:
                        pe.wait_ge(s_tlo, 2 * n - 1 + g)
                    for q in range(TC):
                        js = slice((TC * g + q) * P, (TC * g + q + 1) * P)
                        mm = pe.transpose(PT[:, js], t[j % 2][:, js], ident[:, :])
                    mm.then_inc(s_tr, 1)

            def values(b, par, k, start):
                n = NT * b + k
                if k == 0:
                    pe.wait_ge(s_plo, PJ * (b + 1))
                pe.wait_ge(s_tlo, 2 * n + 2)
                if not start:
                    pe.wait_ge(s_z, n)
                hi, lo = pT[k % 2]
                for j in range(NT):
                    js = slice(j * P, (j + 1) * P)
                    pe.matmul(O[:, 0:DE], hi[:, js], hn[par][0][:, j, :], start=(j == 0), stop=False)
                    pe.matmul(O[:, 0:DE], lo[:, js], hn[par][0][:, j, :], start=False, stop=False)
                    mm = pe.matmul(O[:, 0:D], hi[:, js], hn[par][1][:, j, :], start=False, stop=(j == NT - 1))
                mm.then_inc(s_pv, 1)

            for p in range(PJ):
                project(0, 0, p, True)
            scores(0, 0, 0, True)
            scores(0, 0, 1, True)
            transpose_probs(0, 0, True)

            def emit(b, par, first, last):
                for k in range(NT):
                    if not last:
                        project(b + 1, 1 - par, 2 * k, False)
                    if not (last and k + 2 >= NT):
                        scores(b + (k + 2) // NT, par if k + 2 < NT else 1 - par, (k + 2) % NT, False)
                    if not last:
                        project(b + 1, 1 - par, 2 * k + 1, False)
                    if not (last and k + 1 >= NT):
                        transpose_probs(b + (k + 1) // NT, (k + 1) % NT, False)
                    values(b, par, k, first and k == 0)

            batches(emit, pe.Fori)


class Layers:
    pass


def layer_buffers(nc, ctx, x, w1, rows, s_rows):
    B, N, D, F, NT, KD, KF = shapes(x, w1)
    L = Layers()

    def sb(name, shape, dt=F32):
        return ctx.enter_context(nc.sbuf_tensor(name, shape, dt))

    def ps(name, cols):
        return ctx.enter_context(nc.psum_tensor(name, [P, cols], F32))

    def sem(name):
        return ctx.enter_context(nc.semaphore(name))

    LAYERS = w1.shape[0]
    DE = D + 2
    TC = BANK // P
    L.ident = sb("ident", [P, P])
    L.half = sb("half", [P, TC])
    L.eps = sb("eps", [P, TC])
    L.w1 = [sb("w1_hi", [P, KD, F], F32R), sb("w1_lo", [P, KD, F], F32R)]
    L.w2 = [sb("w2_hi", [P, KF, D], F32R), sb("w2_lo", [P, KF, D], F32R)]
    L.b1 = sb("b1", [P, LAYERS, KF])
    L.b2 = sb("b2", [P, LAYERS, KD])
    L.g1 = sb("g1", [P, LAYERS, KD])
    L.be1 = sb("be1", [P, LAYERS, KD])
    L.g2 = sb("g2", [P, D])
    L.be2 = sb("be2", [P, D])
    L.aw = sb("aw", [P, 2, D])
    L.ab = sb("ab", [P, 1])
    L.mask = [sb(f"mask{i}", [P, N], BF16) for i in range(TC)]
    L.x = rows
    L.x_hi = sb("x_hi", [P, 2, NT, DE], F32R)
    L.x_lo = sb("x_lo", [P, 2, NT, D], F32R)
    L.prod = sb("prod", [P, 2, D])
    L.si = sb("si", [P, NT])
    L.sj = sb("sj", [P, NT])
    L.a8 = sb("a8", [P, NT])
    L.sj_row = sb("sj_row", [P, 2, N])
    L.t = [sb(f"t{i}", [P, N]) for i in range(TC)]
    L.mx = sb("mx", [P, TC])
    L.nmx = sb("nmx", [P, TC])
    L.pT = [[sb(f"pT_hi{i}", [P, N], F32R), sb(f"pT_lo{i}", [P, N], F32R)] for i in range(2)]
    L.rinv = sb("rinv", [P, 1])
    L.u = sb("u", [P, 2, D])
    L.st = sb("st", [P, 2, 6])
    L.mv = sb("mv", [P, 2, 2])
    L.ve = sb("ve", [P, 2])
    L.rstd = sb("rstd", [P, 2])
    L.n1 = sb("n1", [P, 2, TC, D])
    L.h = sb("h", [P, KD, BANK])
    L.h_hi = sb("h_hi", [P, KD, BANK], F32R)
    L.h_lo = sb("h_lo", [P, KD, BANK], F32R)
    L.g = sb("g", [P, G_RING, BANK])
    L.g_hi = sb("g_hi", [P, KF, BANK], F32R)
    L.g_lo = sb("g_lo", [P, KF, BANK], F32R)
    L.rT = sb("rT", [P, KD, BANK])
    L.st2 = sb("st2", [P, TC, 6])
    L.mv2 = sb("mv2", [P, TC, 2])
    L.ve2 = sb("ve2", [P, TC])
    L.rstd2 = sb("rstd2", [P, TC])
    L.xo = sb("xo", [P, TC, D])
    L.x1 = sb("x1", [P, TC, D])
    L.x1_rows = L.x1[:, :, :].rearrange("p t d -> p (t d)")

    L.PT = ps("PT", N)
    L.A = ps("A", BANK)
    L.G = [ps(f"G{i}", BANK) for i in range(2)]
    L.Y = ps("Y", BANK)
    L.G.append(L.Y)
    L.M = ps("M", 2 * BANK)

    L.s_ident = sem("ident")
    L.s_half = sem("half")
    L.s_ones = sem("ones")
    L.s_vec = sem("vec")
    L.s_g2 = sem("g2")
    L.s_aw = sem("aw")
    L.s_w_in = sem("w_in")
    L.s_w_hi = sem("w_hi")
    L.s_w_lo = sem("w_lo")
    L.s_x_in = s_rows
    L.s_x_hi = sem("x_hi")
    L.s_x_lo = sem("x_lo")
    L.s_sj = sem("sj")
    L.s_prep = sem("prep")
    L.s_sjT = sem("sjT")
    L.s_sj_row = sem("sj_row")
    L.s_score = sem("score")
    L.s_masked = sem("masked")
    L.s_nmx = sem("nmx")
    L.s_probs = sem("probs")
    L.s_tr = sem("tr")
    L.s_pt_hi = sem("pt_hi")
    L.s_pt_lo = sem("pt_lo")
    L.s_agg = sem("agg")
    L.s_ln = sem("ln")
    L.s_rs = sem("rs")
    L.s_n1 = sem("n1")
    L.s_hT = sem("hT")
    L.s_h = sem("h")
    L.s_h_lo = sem("h_lo")
    L.s_ffn1 = sem("ffn1")
    L.s_gelu = sem("gelu")
    L.s_g_lo = sem("g_lo")
    L.s_ffn2 = sem("ffn2")
    L.s_res = sem("res")
    L.s_rt = sem("rt")
    L.s_ln2 = sem("ln2")
    L.s_rs2 = sem("rs2")
    L.s_n2 = sem("n2")
    L.s_xo = sem("xo")
    L.s_xst = sem("xst")
    L.s_x1_in = sem("x1_in")
    L.s_fin = sem("fin")
    L.s_passed = sem("passed")
    L.s_mask = [sem(f"mask_in{i}") for i in range(TC)]
    return L


def graph_layers(nc, L, x, rows, x1, out, mask, par):
    attn_w, attn_b, W1, b1, W2, b2, g1, be1, g2, be2 = par
    B, N, D, F, NT, KD, KF = shapes(x, W1)
    LAYERS = W1.shape[0]
    DE, TC = D + 2, BANK // P
    NCH = N // BANK
    C = B * NCH
    U = B * NT
    assert NCH == 2 and NT == NCH * TC and KF == NT and B % 2 == 0
    W_STEPS = (1, 2, 3, 4)
    lo_beside = {2: range(NT // 2), 3: range(NT // 2, NT)}

    def bases(layer):
        return layer * U, layer * C, layer * B

    def before(layer, c, n):
        return layer == 0 and isinstance(c, int) and c < n

    def of_last(layer, c):
        return layer == LAYERS - 1 and not (isinstance(c, int) and c < 0)

    def owner(layer, c):
        return layer - 1 if isinstance(c, int) and c < 0 else layer

    def weight_half(part, i):
        if i < 2:
            return L.w1[part][:, i, :]
        return L.w2[part][:, (i - 2) * KF // 2:(i - 1) * KF // 2, :].rearrange("p f d -> p (f d)")

    def last_used(eng, c0, i):
        eng.wait_ge(L.s_ffn1 if i < 2 else L.s_ffn2, KF * c0 if i < 2 else KD * c0)

    def scale_shift(eng, k):
        eng.wait_ge(L.s_n2, k + 1)
        eng.tensor_tensor(L.xo[:, :, :], L.xo[:, :, :], L.g2[:, :].unsqueeze(1).to_broadcast([P, TC, D]),
                          ALU.mult).then_inc(L.s_xo, 1)
        eng.wait_ge(L.s_xo, 2 * k + 1)
        eng.tensor_tensor(L.xo[:, :, :], L.xo[:, :, :], L.be2[:, :].unsqueeze(1).to_broadcast([P, TC, D]),
                          ALU.add).then_inc(L.s_xo, 1)

    def add_x1(eng, c0, k):
        eng.wait_ge(L.s_x1_in, 16 * (k + 1))
        eng.wait_ge(L.s_xo, 2 * (c0 + k + 1))
        eng.tensor_tensor(L.xo[:, :, :], L.xo[:, :, :], L.x1[:, :, :], ALU.add).then_inc(L.s_fin, 1)

    def rs2(layer, c, final):
        c0 = layer * C
        return 2 * c0 + (4 * c + 2 * final if of_last(layer, c) else 2 * c)

    def batches(layer, emit, loop, last_apart=False):
        for b in range(2):
            for h in range(NCH):
                c = NCH * b + h
                emit(b, h, True, not before(layer, c, 1), not before(layer, c, 2), not before(layer, c, 3))
        with loop(2, B - last_apart) as b:
            for h in range(NCH):
                emit(b, h, True, True, True, True)
        if last_apart:
            for h in range(NCH):
                emit(B - 1, h, True, True, True, True)
        if layer == LAYERS - 1:
            emit(B, 0, False, True, True, True)
            emit(B, 1, False, False, True, True)
            emit(B + 1, 0, False, False, False, True)

    with nc.Block() as block:
        @block.sync
        def _(sp):
            def load_x(row, par):
                sp.dma_start(L.x[:, par, :, :].rearrange("p (c t) d -> p c t d", c=NCH),
                             rows[bass.ds(row, NCH)].rearrange("c p t d -> p c t d")).then_inc(L.s_x_in, 16)

            def load_mask(b, s):
                sp.dma_start(L.mask[s % TC][:, :], mask[b * NT + s % NT]).then_inc(L.s_mask[s % TC], 16)

            def load_attention(layer):
                for dst, src in ((L.aw[:, 0, :], attn_w[layer, 0:D]), (L.aw[:, 1, :], attn_w[layer, D:2 * D])):
                    sp.dma_start(dst, src.partition_broadcast(P)).then_inc(L.s_aw, 16)
                sp.dma_start(L.ab[:, :], attn_b[layer:layer + 1].partition_broadcast(P)).then_inc(L.s_aw, 16)

            def load_norm2(layer):
                sp.dma_start(L.g2[:, :], g2[layer].partition_broadcast(P)).then_inc(L.s_g2, 16)
                sp.dma_start(L.be2[:, :], be2[layer].partition_broadcast(P)).then_inc(L.s_g2, 16)

            def load_columns():
                with nc.allow_non_contiguous_dma("columns of the layers' vectors"):
                    for dst, src in ((L.b1, b1), (L.b2, b2), (L.g1, g1), (L.be1, be1)):
                        for layer in range(LAYERS):
                            sp.dma_start(dst[:, layer, :], src[layer].rearrange("(k p) -> p k", p=P)).then_inc(L.s_vec, 16)

            load_attention(0)
            for s in range(TC):
                load_mask(0, s)

            def one_layer(layer):
                u0, c0, n0 = bases(layer)

                def emit(b, h, att, ffn, rt, old):
                    u, c = NT * b + TC * h, NCH * b + h
                    if att and h == 0:
                        if not before(layer, c, 1):
                            sp.wait_ge(L.s_ln, 4 * (u0 + u))
                        sp.wait_ge(L.s_x_in, 16 * (n0 + b + 1))
                        last_batch = isinstance(b, int) and b == B - 1
                        if layer > 0 or last_batch:
                            sp.wait_ge(L.s_xst, 16 * (c0 - C + NCH * (b + 2)))
                        end = layer == LAYERS - 1 and last_batch
                        load_x(0 if end else c0 + NCH * (b + 1), (b + 1) % 2)
                        sp.wait_ge(L.s_prep, 2 * (n0 + b + 1))
                        load_attention(layer if end or not last_batch else layer + 1)
                        if before(layer, c, 1):
                            load_columns()
                    if old and of_last(layer, c - 3):
                        if isinstance(c, int) and c == 3:
                            sp.wait_ge(L.s_w_lo, 4 * LAYERS)
                        else:
                            sp.wait_ge(L.s_fin, 4 * (c - 3))
                        sp.dma_start(L.x1[:, :, :], x1[c - 3]).then_inc(L.s_x1_in, 16)
                    if att:
                        for q in range(TC):
                            s = TC * h + q
                            sp.wait_ge(L.s_masked, u0 + u + q + 1)
                            load_mask(b if h == 0 else (b + 1) % B, s + TC)
                            if q == 1 and old:
                                store(c - 3)
                            if isinstance(c, int) and c < 2 and s in W_STEPS:
                                load_weight(W_STEPS.index(s))
                    elif old:
                        store(c - 3)
                    if att and isinstance(c, int) and c == 2:
                        if layer > 0:
                            sp.wait_ge(L.s_xo, 2 * c0)
                        load_norm2(layer)

                def load_weight(i):
                    if not (layer == 0 and i == 0):
                        sp.wait_ge(L.s_w_lo, 4 * layer + i)
                    if i < 2:
                        dst, src = L.x1_rows, W1[layer, i * P:(i + 1) * P, :]
                    else:
                        half = W2[layer].rearrange("(f p) d -> p f d", p=P)
                        dst, src = L.x1[:, :, :], half[:, (i - 2) * KF // 2:(i - 1) * KF // 2, :]
                    sp.dma_start(dst, src).then_inc(L.s_w_in, 16)

                def store(k):
                    if of_last(layer, k):
                        sp.wait_ge(L.s_fin, 4 * (k + 1))
                        dst = out[k]
                    else:
                        sp.wait_ge(L.s_xo, 2 * (c0 + k + 1))
                        dst = rows[c0 + C + k]
                    sp.dma_start(dst, L.xo[:, :, :]).then_inc(L.s_xst, 16)

                batches(layer, emit, sp.Fori, last_apart=True)

            for layer in range(LAYERS):
                one_layer(layer)
            sp.wait_ge(L.s_xst, 16 * LAYERS * C)
            sp.wait_ge(L.s_x_in, 16 * (LAYERS * B + 1))
            sp.wait_ge(L.s_aw, 48 * (LAYERS * B + 1))
            for i in range(TC):
                sp.wait_ge(L.s_mask[i], 16 * (LAYERS * U + TC) // TC)

        @block.gpsimd
        def _(pool):
            make_identity(pool, L.ident, L.s_ident)
            pool.memset(L.half[:, :], -0.5).then_inc(L.s_half, 1)
            pool.memset(L.eps[:, :], EPS).then_inc(L.s_half, 1)
            for i in range(2):
                pool.memset(L.x_hi[:, i, :, D:D + 1].bitcast(F32), 1.0).then_inc(L.s_ones, 1)
                pool.memset(L.x_hi[:, i, :, D + 1:DE].bitcast(F32), 0.0).then_inc(L.s_ones, 1)
            pool.wait_ge(L.s_half, 2)

            def one_layer(layer):
                u0, c0, n0 = bases(layer)
                def x_lo(n, par, v):
                    pool.wait_ge(L.s_x_hi, NT * (n0 + n) + v + 1)
                    pool.tensor_tensor(L.x_lo[:, par, v, :], L.x[:, par, v, :], L.x_hi[:, par, v, 0:D].bitcast(F32),
                                       ALU.subtract).then_inc(L.s_x_lo, 1)

                if layer == 0:
                    for v in range(NT):
                        x_lo(0, 0, v)

                def deviation(u, i):
                    pool.wait_ge(L.s_ln, 4 * (u0 + u + 1))
                    pool.tensor_tensor(L.ve[:, i:i + 1], L.mv[:, i, 1:2], L.eps[:, 0:1], ALU.add).then_inc(L.s_rs, 1)
                    pool.wait_ge(L.s_rs, 2 * (u0 + u) + 1)
                    pool.tensor_tensor(L.rstd[:, i:i + 1], L.ve[:, i:i + 1], L.half[:, 0:1], ALU.pow).then_inc(L.s_rs, 1)

                def final_rstd(k):
                    pool.wait_ge(L.s_fin, 4 * k + 3)
                    pool.tensor_tensor(L.ve2[:, :], L.mv2[:, :, 1], L.eps[:, :], ALU.add).then_inc(L.s_rs2, 1)
                    pool.wait_ge(L.s_rs2, rs2(layer, k, 1) + 1)
                    pool.tensor_tensor(L.rstd2[:, :], L.ve2[:, :], L.half[:, :], ALU.pow).then_inc(L.s_rs2, 1)

                def emit(b, h, att, ffn, rt, old):
                    u, c = NT * b + TC * h, NCH * b + h
                    final = old and of_last(layer, c - 3)
                    for q in range(TC):
                        s = TC * h + q
                        if q == 1 and final and (att or ffn):
                            add_x1(pool, c0, c - 3)
                        if q == 0 and ffn:
                            for k in range(KD):
                                pool.wait_ge(L.s_h, 2 * (KD * (c0 + c - 1) + k + 1))
                                pool.tensor_tensor(L.h_lo[:, k, :], L.h[:, k, :], L.h_hi[:, k, :].bitcast(F32),
                                                   ALU.subtract).then_inc(L.s_h_lo, 1)
                        if att and not (q == 1 and ffn):
                            deviation(u + q, q % 2)
                        if q == 1 and final and not ffn:
                            final_rstd(c - 3)
                        if q == 1 and ffn:
                            for f in range(KF):
                                if f == 2 and att:
                                    deviation(u + q, q % 2)
                                if f == KF // 2 and final:
                                    final_rstd(c - 3)
                                pool.wait_ge(L.s_gelu, 2 * (KF * (c0 + c - 1) + f + 1))
                                pool.tensor_tensor(L.g_lo[:, f, :], L.g[:, f % G_RING, :], L.g_hi[:, f, :].bitcast(F32),
                                                   ALU.subtract).then_inc(L.s_g_lo, 1)
                        if q == 2 and rt:
                            k = c0 + c - 2
                            pool.wait_ge(L.s_ln2, 2 * TC * (k + 1))
                            pool.tensor_tensor(L.ve2[:, :], L.mv2[:, :, 1], L.eps[:, :], ALU.add).then_inc(L.s_rs2, 1)
                            pool.wait_ge(L.s_rs2, rs2(layer, c - 2, 0) + 1)
                            pool.tensor_tensor(L.rstd2[:, :], L.ve2[:, :], L.half[:, :], ALU.pow).then_inc(L.s_rs2, 1)
                        if att:
                            for v in lo_beside.get(s, ()):
                                x_lo(b + 1, (b + 1) % 2, v)
                        if q == 3 and rt and att:
                            if isinstance(c, int) and c == 2:
                                pool.wait_ge(L.s_g2, 32 * (layer + 1))
                            scale_shift(pool, c0 + c - 2)

                batches(layer, emit, pool.Fori)

            for layer in range(LAYERS):
                one_layer(layer)

        @block.scalar
        def _(act):
            def one_layer(layer):
                u0, c0, n0 = bases(layer)
                def weights_hi(i):
                    if layer > 0:
                        last_used(act, c0, i)
                    act.wait_ge(L.s_w_in, 16 * (4 * layer + i + 1))
                    act.activation(weight_half(0, i), L.x1_rows, ACT.Copy).then_inc(L.s_w_hi, 1)

                def pt_hi(u, i, first):
                    if not first:
                        act.wait_ge(L.s_agg, u0 + u - 1)
                    for g in range(2):
                        act.wait_ge(L.s_tr, 2 * (u0 + u) + g + 1)
                        gs = slice(g * BANK, (g + 1) * BANK)
                        act.activation(L.pT[i][0][:, gs], L.PT[:, gs], ACT.Copy).then_inc(L.s_pt_hi, 1)

                def exp(u, s):
                    i = s % TC
                    act.wait_ge(L.s_nmx, u0 + u + 1)
                    act.activation(L.t[i][:, :], L.t[i][:, :], ACT.Exp, bias=L.nmx[:, i:i + 1]).then_inc(L.s_probs, 1)

                def sj_row(n):
                    act.wait_ge(L.s_sjT, n0 + n + 1)
                    if not (layer == 0 and isinstance(n, int) and n == 0):
                        act.wait_ge(L.s_score, u0 + NT * n)
                    act.activation(L.sj_row[:, 0, :], L.M[:, :], ACT.Copy).then_inc(L.s_sj_row, 1)

                if layer == 0:
                    sj_row(0)
                    for s in range(AHEAD - 1):
                        exp(s, s)
                    pt_hi(0, 0, True)

                def emit(b, h, att, ffn, rt, old):
                    u, c = NT * b + TC * h, NCH * b + h
                    for q in range(TC):
                        s = TC * h + q
                        if att:
                            pt_hi(u + q + 1, (q + 1) % 2, before(layer, c, 1) and s == 0)
                        if q == 0 and ffn:
                            k0 = KD * (c0 + c - 1)
                            if before(layer, c, 2):
                                act.wait_ge(L.s_vec, 16 * 4 * LAYERS)
                            if not before(layer, c, 2):
                                act.wait_ge(L.s_res, k0)
                            for k in range(KD):
                                act.wait_ge(L.s_hT, k0 + k + 1)
                                for dst in (L.h, L.h_hi):
                                    act.activation(dst[:, k, :], L.M[:, k * BANK:(k + 1) * BANK], ACT.Identity,
                                                   bias=L.be1[:, owner(layer, c - 1), k:k + 1],
                                                   scale=L.g1[:, owner(layer, c - 1), k:k + 1]).then_inc(L.s_h, 1)
                        if att:
                            exp(u + q + 2, s + 2)
                            if s == TC:
                                sj_row(b + 1)
                        if q == 1 and ffn:
                            k0 = KF * (c0 + c - 1)
                            if not before(layer, c, 2):
                                act.wait_ge(L.s_ffn2, KD * (c0 + c - 1))
                            for f in range(KF):
                                act.wait_ge(L.s_ffn1, k0 + f + 1)
                                if f >= G_RING:
                                    act.wait_ge(L.s_g_lo, k0 + f + 1 - G_RING)
                                for dst in (L.g[:, f % G_RING, :], L.g_hi[:, f, :]):
                                    act.activation(dst, L.G[f % 3][:, :], ACT.Gelu, bias=L.b1[:, owner(layer, c - 1), f:f + 1])\
                                       .then_inc(L.s_gelu, 1)

                        if att and isinstance(c, int) and c < 2 and s - 1 in W_STEPS:
                            weights_hi(W_STEPS.index(s - 1))

                batches(layer, emit, act.Fori)

            for layer in range(LAYERS):
                one_layer(layer)

        @block.vector
        def _(dve):
            def one_layer(layer):
                u0, c0, n0 = bases(layer)
                def weights_lo(i):
                    dve.wait_ge(L.s_w_hi, 4 * layer + i + 1)
                    dve.tensor_tensor(weight_half(1, i), L.x1_rows, weight_half(0, i).bitcast(F32), ALU.subtract)\
                       .then_inc(L.s_w_lo, 1)

                def prep_tile(n, par, v):
                    if v == 0:
                        dve.wait_ge(L.s_x_in, 16 * (n0 + n + 1))
                        dve.wait_ge(L.s_aw, 48 * (n0 + n + 1))
                    dve.tensor_copy(L.x_hi[:, par, v, 0:D], L.x[:, par, v, :]).then_inc(L.s_x_hi, 1)
                    for half, dst in ((0, L.si), (1, L.sj)):
                        if 2 * v + half >= 2:
                            dve.wait_ge(L.s_sj, 2 * (NT * (n0 + n) + v) + half - 1)
                        dve.scalar_tensor_tensor(L.prod[:, half, :], L.x[:, par, v, :], 1.0, L.aw[:, half, :], ALU.mult,
                                                 ALU.mult, accum_out=dst[:, v:v + 1]).then_inc(L.s_sj, 1)

                def prep_batch(n, first):
                    dve.wait_ge(L.s_sj, 2 * NT * (n0 + n + 1))
                    if not first:
                        dve.wait_ge(L.s_score, u0 + NT * n)
                    dve.tensor_scalar(L.a8[:, :], L.si[:, :], L.ab[:, :], 1.0 - SLOPE, ALU.add, ALU.mult).then_inc(L.s_prep, 1)
                    dve.wait_ge(L.s_sj_row, n0 + n + 1)
                    dve.tensor_scalar(L.sj_row[:, 1, :], L.sj_row[:, 0, :], SLOPE, None, ALU.mult).then_inc(L.s_prep, 1)
                    dve.wait_ge(L.s_prep, 2 * (n0 + n + 1))

                def masked(u, s, k):
                    i = s % TC
                    t = L.t[i][:, :]
                    if not (layer == 0 and isinstance(u, int) and u < TC):
                        dve.wait_ge(L.s_tr, 2 * (u0 + u + 1 - TC))
                    dve.scalar_tensor_tensor(t, L.sj_row[:, 0, :], L.a8[:, s:s + 1], L.sj_row[:, 1, :], ALU.add,
                                             ALU.max).then_inc(L.s_score, 1)
                    wait_alone(dve, L.s_passed, (L.s_score, u0 + u + 1), (L.s_mask[i], 16 * (u0 // TC + k + 1)))
                    dve.tensor_tensor_reduce(out=t, in0=t, in1=L.mask[i][:, :], scale=1.0, scalar=LOWEST, op0=ALU.add,
                                             op1=ALU.max, accum_out=L.mx[:, i:i + 1]).then_inc(L.s_masked, 1)
                    dve.wait_ge(L.s_masked, u0 + u + 1)
                    dve.tensor_scalar(L.nmx[:, i:i + 1], L.mx[:, i:i + 1], -1.0, None, ALU.mult).then_inc(L.s_nmx, 1)

                def pt_lo(u, i):
                    for g in range(2):
                        dve.wait_ge(L.s_pt_hi, 2 * (u0 + u) + g + 1)
                        gs = slice(g * BANK, (g + 1) * BANK)
                        dve.tensor_tensor(L.pT[i][1][:, gs], L.PT[:, gs], L.pT[i][0][:, gs].bitcast(F32), ALU.subtract)\
                           .then_inc(L.s_pt_lo, 1)

                def norm1_stats(u, s, par):
                    i = s % 2
                    n = 4 * (u0 + u)
                    dve.wait_ge(L.s_agg, u0 + u + 1)
                    dve.reciprocal(L.rinv[:, :], L.A[:, D:D + 1]).then_inc(L.s_ln, 1)
                    dve.wait_ge(L.s_ln, n + 1)
                    if not (layer == 0 and isinstance(u, int) and u < 2):
                        dve.wait_ge(L.s_n1, u0 + u - 1)
                    dve.scalar_tensor_tensor(L.u[:, i, :], L.A[:, 0:D], L.rinv[:, :], L.x[:, par, s, :], ALU.mult, ALU.add)\
                       .then_inc(L.s_ln, 1)
                    dve.wait_ge(L.s_ln, n + 2)
                    dve.bn_stats(L.st[:, i, :], L.u[:, i, :]).then_inc(L.s_ln, 1)
                    wait_alone(dve, L.s_passed, (L.s_ln, n + 3))
                    dve.bn_aggr(L.mv[:, i, :], L.st[:, i, :]).then_inc(L.s_ln, 1)

                def norm1_rows(u, h, q):
                    i = q % 2
                    dve.wait_ge(L.s_rs, 2 * (u0 + u + 1))
                    dve.tensor_scalar(L.n1[:, h, q, :], L.u[:, i, :], L.mv[:, i, 0:1], L.rstd[:, i:i + 1], ALU.subtract,
                                      ALU.mult).then_inc(L.s_n1, 1)

                if layer == 0:
                    for v in range(NT):
                        prep_tile(0, 0, v)
                    prep_batch(0, True)
                    for s in range(AHEAD):
                        masked(s, s, 0)
                    pt_lo(0, 0)

                def emit(b, h, att, ffn, rt, old):
                    u, c = NT * b + TC * h, NCH * b + h
                    final = old and of_last(layer, c - 3)
                    for q in range(TC):
                        s = TC * h + q
                        if q == 2 and rt:
                            k = c0 + c - 2
                            dve.wait_ge(L.s_rt, k + 1)
                            for t in range(TC):
                                dve.bn_stats(L.st2[:, t, :], L.M[:, t * D:(t + 1) * D]).then_inc(L.s_ln2, 1)
                            wait_alone(dve, L.s_passed, (L.s_ln2, 2 * TC * k + TC))
                            for t in range(TC):
                                dve.bn_aggr(L.mv2[:, t, :], L.st2[:, t, :]).then_inc(L.s_ln2, 1)
                        if q == 3 and rt:
                            k = c0 + c - 2
                            dve.wait_ge(L.s_rs2, rs2(layer, c - 2, 0) + 2)
                            if not before(layer, c, 3):
                                dve.wait_ge(L.s_xst, 16 * k)
                            for t in range(TC):
                                mm = dve.tensor_scalar(L.xo[:, t, :], L.M[:, t * D:(t + 1) * D], L.mv2[:, t, 0:1],
                                                       L.rstd2[:, t:t + 1], ALU.subtract, ALU.mult)
                            mm.then_inc(L.s_n2, 1)
                            if not att:
                                dve.wait_ge(L.s_g2, 32 * LAYERS)
                                scale_shift(dve, k)
                        if att:
                            v = s + AHEAD
                            if v == NT:
                                prep_batch(b + 1, False)
                            if q < 3:
                                masked(u + q + AHEAD, v % NT, NCH * b + v // TC)
                            pt_lo(u + q + 1, (q + 1) % 2)
                            if q >= 1:
                                norm1_rows(u + q - 1, h, q - 1)
                            norm1_stats(u + q, s, b % 2)
                            if q == 3:
                                masked(u + q + AHEAD, v % NT, NCH * b + v // TC)
                                norm1_rows(u + q, h, q)
                        if q == 1 and final:
                            if not (att or ffn):
                                add_x1(dve, c0, c - 3)
                            dve.wait_ge(L.s_fin, 4 * (c - 3) + 1)
                            for t in range(TC):
                                mm = dve.bn_stats(L.st2[:, t, :], L.xo[:, t, :])
                            mm.then_inc(L.s_fin, 1)
                            wait_alone(dve, L.s_passed, (L.s_fin, 4 * (c - 3) + 2))
                            for t in range(TC):
                                mm = dve.bn_aggr(L.mv2[:, t, :], L.st2[:, t, :])
                            mm.then_inc(L.s_fin, 1)
                        if att and s == 1:
                            for v in range(NT):
                                prep_tile(b + 1, (b + 1) % 2, v)
                        if q == 1 and final:
                            dve.wait_ge(L.s_rs2, rs2(layer, c - 3, 1) + 2)
                            for t in range(TC):
                                mm = dve.tensor_scalar(L.xo[:, t, :], L.xo[:, t, :], L.mv2[:, t, 0:1], L.rstd2[:, t:t + 1],
                                                       ALU.subtract, ALU.mult)
                            mm.then_inc(L.s_fin, 1)
                        if q >= 2 and ffn:
                            k = q - 2
                            n = KD * (c0 + c - 1) + k
                            if before(layer, c, 2) and k == 0:
                                dve.wait_ge(L.s_vec, 16 * 4 * LAYERS)
                            dve.wait_ge(L.s_ffn2, n + 1)
                            if not before(layer, c, 2):
                                dve.wait_ge(L.s_rt, c0 + c - 1)
                            dve.scalar_tensor_tensor(L.rT[:, k, :], L.Y[:, :], L.b2[:, owner(layer, c - 1), k:k + 1], L.h[:, k, :], ALU.add,
                                                     ALU.add).then_inc(L.s_res, 1)
                        if att and isinstance(c, int) and c < 2 and s - 1 in W_STEPS:
                            weights_lo(W_STEPS.index(s - 1))

                batches(layer, emit, dve.Fori)

            for layer in range(LAYERS):
                one_layer(layer)

        @block.tensor
        def _(pe):
            pe.wait_ge(L.s_ident, 2)
            pe.wait_ge(L.s_ones, 4)

            def one_layer(layer):
                u0, c0, n0 = bases(layer)
                def transpose_probs(u, s, first):
                    pe.wait_ge(L.s_probs, u0 + u + 1)
                    for g in range(2):
                        if not first:
                            pe.wait_ge(L.s_pt_lo, 2 * (u0 + u) - 1 + g)
                        for q in range(TC):
                            js = slice((TC * g + q) * P, (TC * g + q + 1) * P)
                            mm = pe.transpose(L.PT[:, js], L.t[s % TC][:, js], L.ident[:, :])
                        mm.then_inc(L.s_tr, 1)

                def aggregate(u, i, b, par, first):
                    pe.wait_ge(L.s_pt_lo, 2 * (u0 + u + 1))
                    if not first:
                        pe.wait_ge(L.s_ln, 4 * (u0 + u) - 2)
                    for j in range(NT):
                        js = slice(j * P, (j + 1) * P)
                        hi, lo = L.pT[i][0][:, js], L.pT[i][1][:, js]
                        pe.matmul(L.A[:, 0:DE], hi, L.x_hi[:, par, j, :], start=(j == 0), stop=False)
                        pe.matmul(L.A[:, 0:DE], lo, L.x_hi[:, par, j, :], start=False, stop=False)
                        mm = pe.matmul(L.A[:, 0:D], hi, L.x_lo[:, par, j, :], start=False, stop=(j == NT - 1))
                    mm.then_inc(L.s_agg, 1)

                def sj_row(n):
                    pe.wait_ge(L.s_sj, 2 * NT * (n0 + n + 1))
                    for v in range(NT):
                        mm = pe.transpose(L.M[:, v * P:(v + 1) * P], L.sj[:, v:v + 1].to_broadcast([P, P]), L.ident[:, :])
                    mm.then_inc(L.s_sjT, 1)

                if layer == 0:
                    sj_row(0)
                    transpose_probs(0, 0, True)

                def emit(b, h, att, ffn, rt, old):
                    u, c = NT * b + TC * h, NCH * b + h
                    start = before(layer, c, 1)
                    for q in range(TC):
                        s = TC * h + q
                        if att:
                            transpose_probs(u + q + 1, q + 1, False)
                        if q == 0 and ffn:
                            k0 = c0 + c - 1
                            pe.wait_ge(L.s_n1, TC * (k0 + 1))
                            if before(layer, c, 3):
                                pe.wait_ge(L.s_sj_row, n0 + c)
                            else:
                                pe.wait_ge(L.s_n2, k0 - 1)
                            for k in range(KD):
                                for t in range(TC):
                                    mm = pe.transpose(L.M[:, k * BANK + t * P:k * BANK + (t + 1) * P],
                                                      L.n1[:, (h + 1) % 2, t, k * P:(k + 1) * P], L.ident[:, :])
                                mm.then_inc(L.s_hT, 1)
                        if att:
                            if s == 0:
                                pe.wait_ge(L.s_x_lo, NT * (n0 + b + 1))
                            aggregate(u + q, q % 2, b, b % 2, start and q == 0)
                            if s == TC:
                                pe.wait_ge(L.s_h, 2 * KD * (c0 + c))
                                sj_row(b + 1)
                        if q == 1 and ffn:
                            k0 = c0 + c - 1
                            pe.wait_ge(L.s_h_lo, KD * (k0 + 1))
                            if isinstance(c, int) and c == 1:
                                pe.wait_ge(L.s_w_lo, 4 * layer + 2)
                            for f in range(KF):
                                n = KF * k0 + f
                                if f >= 3:
                                    pe.wait_ge(L.s_gelu, 2 * (n - 2))
                                elif not before(layer, c, 2):
                                    if f == 2:
                                        pe.wait_ge(L.s_res, KD * k0)
                                    else:
                                        pe.wait_ge(L.s_gelu, 2 * KF * k0)
                                fs = slice(f * P, (f + 1) * P)
                                for k in range(KD):
                                    mm = split_product(pe, L.G[f % 3][:, :], (L.w1[0][:, k, fs], L.w1[1][:, k, fs]),
                                                       (L.h_hi[:, k, :], L.h_lo[:, k, :]), k == 0, k == KD - 1)
                                mm.then_inc(L.s_ffn1, 1)
                        if q == 1 and rt:
                            k0 = c0 + c - 2
                            if att and h == 1:
                                pe.wait_ge(L.s_sj_row, n0 + b + 2)
                            elif ffn:
                                pe.wait_ge(L.s_h, 2 * KD * (k0 + 2))
                            else:
                                pe.wait_ge(L.s_n2, k0)
                            pe.wait_ge(L.s_res, KD * (k0 + 1))
                            for t in range(TC):
                                for k in range(KD):
                                    mm = pe.transpose(L.M[:, t * D + k * P:t * D + (k + 1) * P],
                                                      L.rT[:, k, t * P:(t + 1) * P], L.ident[:, :])
                            mm.then_inc(L.s_rt, 1)
                        if q >= 2 and ffn:
                            k0 = c0 + c - 1
                            o = q - 2
                            pe.wait_ge(L.s_g_lo, KF * (k0 + 1))
                            if o == 0:
                                pe.wait_ge(L.s_gelu, 2 * KF * (k0 + 1))
                            else:
                                pe.wait_ge(L.s_res, KD * k0 + o)
                            if isinstance(c, int) and c == 1:
                                pe.wait_ge(L.s_w_lo, 4 * layer + 4)
                            os = slice(o * P, (o + 1) * P)
                            for f in range(KF):
                                mm = split_product(pe, L.Y[:, :], (L.w2[0][:, f, os], L.w2[1][:, f, os]),
                                                   (L.g_hi[:, f, :], L.g_lo[:, f, :]), f == 0, f == KF - 1)
                            mm.then_inc(L.s_ffn2, 1)

                batches(layer, emit, pe.Fori)

            for layer in range(LAYERS):
                one_layer(layer)


def program(nc, x, adj, L0_W, L0_b, L0_attn, attn_w, attn_b, W1, b1, W2, b2, g1, beta1, g2, beta2, out):
    B, N, D, _, NT, _, _ = shapes(x, W1)
    TC = BANK // P
    C = B * N // BANK
    layers = W1.shape[0]
    rows = nc.dram_tensor("rows", (layers * C * TC, P, D), F32, kind="Internal").ap()
    mask = nc.dram_tensor("mask", (B * NT, P, N), BF16, kind="Internal").ap()
    chunks = rows.rearrange("(c t) p d -> c p t d", t=TC)
    out_chunks = out.rearrange("b (c t p) d -> (b c) p t d", t=TC, p=P)
    par = (attn_w, attn_b, W1, b1, W2, b2, g1, beta1, g2, beta2)
    with ExitStack() as ctx:
        x_rows = ctx.enter_context(nc.sbuf_tensor("x_rows", [P, 2, NT, D], F32))
        s_rows = ctx.enter_context(nc.semaphore("x_in"))
        first_stage(nc, x, adj, L0_W, L0_b, L0_attn, rows, mask, W1, x_rows, s_rows)
        L = layer_buffers(nc, ctx, x, W1, x_rows, s_rows)
        graph_layers(nc, L, x, chunks, chunks, out_chunks, mask, par)


_INS = ['x', 'adj', 'L0_gnn_W', 'L0_gnn_b', 'L0_gnn_attn', 'L1_gnn_attn_w', 'L1_gnn_attn_b', 'L1_gnn_W1', 'L1_gnn_b1',
        'L1_gnn_W2', 'L1_gnn_b2', 'L1_gnn_g1', 'L1_gnn_beta1', 'L1_gnn_g2', 'L1_gnn_beta2']


def kernel(**inputs):
    import numpy as _np
    import concourse.bacc as _bacc
    from concourse import mybir as _mybir
    from concourse.bass_utils import run_bass_kernel_spmd as _run

    nc = _bacc.Bacc("TRN2", target_bir_lowering=False, num_devices=1)
    arrays, args = {}, []
    for name in _INS:
        a = _np.ascontiguousarray(inputs[name])
        arrays[f"in_{name}"] = a
        args.append(nc.dram_tensor(f"in_{name}", a.shape, _mybir.dt.from_np(a.dtype), kind="ExternalInput").ap())
    shape = inputs["x"].shape
    args.append(nc.dram_tensor("out_rows", shape, _mybir.dt.float32, kind="ExternalOutput").ap())
    program(nc, *args)
    r = _run(nc, [arrays], core_ids=[0])
    return r.results[0]["out_rows"]
```
